# Optimizing a Trainium2 kernel written in Bass

```python
import numpy as np
import jax
import jax.numpy as jnp

def _softmax(x, axis=-1):
    return jax.nn.softmax(x, axis=axis)

def _gelu(x):
    return jax.nn.gelu(x, approximate=True)

def _silu(x):
    return jax.nn.silu(x)

def _sigmoid(x):
    return jax.nn.sigmoid(x)

def _layernorm(x, axis=-1, eps=1e-05):
    m = jnp.mean(x, axis=axis, keepdims=True)
    v = jnp.var(x, axis=axis, keepdims=True)
    return (x - m) / jnp.sqrt(v + eps)

def _scatter_add(tgt, idx, src, axis=0):
    return tgt.at[idx].add(src)

def _segment_sum(src, seg, n):
    return jax.ops.segment_sum(src, seg, n)
kernel_name = 'mk_decoder_preln_d1_seqx_r8_ddb02a'

def setup_inputs(seed: int=0):
    np.random.seed(seed)
    _w = jnp.asarray

    def _rec_inputs():
        import jax
        import jax.numpy as jnp
        _rk = jax.random.key(seed)
        x = 7.22e-05 + 1 * jax.random.normal(jax.random.fold_in(_rk, 1), (64, 128, 128), jnp.float32)
        _lenS = 128 - jax.random.randint(jax.random.fold_in(_rk, 7), (64,), 0, max(1, 128 // 4) + 1, jnp.int32)
        _lenS2 = 120 - jax.random.randint(jax.random.fold_in(_rk, 8), (64,), 0, max(1, 120 // 4) + 1, jnp.int32)
        _ctx_1024P = jax.random.normal(jax.random.fold_in(_rk, 11), (64, 16, 128), jnp.float32)
        _ctx_1024c = jax.random.dirichlet(jax.random.fold_in(_rk, 511), 0.3 * jnp.ones((16,), jnp.float32), (64, 120))
        _ctx_1024t = jnp.einsum('bsk,bkd->bsd', _ctx_1024c, _ctx_1024P)
        _ctx_1024t = _ctx_1024t * jax.lax.rsqrt(jnp.mean(jnp.square(_ctx_1024t)) + 1e-12) * 0.953939
        ctx_1024 = 4.13588e-05 + 0.999923 * (_ctx_1024t + 0.3 * jax.random.normal(jax.random.fold_in(_rk, 611), (64, 120, 128), jnp.float32))
        return (x, ctx_1024)
    x, ctx_1024 = _rec_inputs()

    def _L0_attn_setup():
        import jax, jax.numpy as jnp
        import numpy as np
        B, S, D = (1, 512, 128)
        H, KV, WIN = (8, 2, 32)
        HD = D // H
        FP16_MIN = -65504.0
        key = jax.random.key(seed)
        ks = jax.random.split(key, 10)
        sc = 0.02
        return {'x': jax.random.normal(ks[0], (B, S, D), dtype=jnp.float32), 'sink_bias': jnp.float32(0.0), 'Wq': jax.random.normal(ks[1], (H * HD, D), dtype=jnp.float32) * sc, 'bq': jnp.zeros((H * HD,), dtype=jnp.float32), 'Wk': jax.random.normal(ks[2], (KV * HD, D), dtype=jnp.float32) * sc, 'bk': jnp.zeros((KV * HD,), dtype=jnp.float32), 'Wv': jax.random.normal(ks[3], (KV * HD, D), dtype=jnp.float32) * sc, 'bv': jnp.zeros((KV * HD,), dtype=jnp.float32), 'Wo': jax.random.normal(ks[4], (D, H * HD), dtype=jnp.float32) * sc, 'bo': jnp.zeros((D,), dtype=jnp.float32)}
    _L0_attn_all = _L0_attn_setup()
    _L0_attn_in = {k: v for k, v in _L0_attn_all.items() if k in ('sink_bias', 'Wq', 'bq', 'Wk', 'bk', 'Wv', 'bv', 'Wo', 'bo')}
    del _L0_attn_all

    def _L0_xattn_setup():
        import jax, jax.numpy as jnp
        import numpy as np
        D_MODEL = 128
        NHEAD = 16
        D_K = D_MODEL // NHEAD
        key = jax.random.key(seed)
        ks = jax.random.split(key, 11)
        B, S = (4, 256)
        s = 1.0 / np.sqrt(D_MODEL)
        return {'query': jax.random.normal(ks[0], (B, S, D_MODEL), jnp.float32), 'key': jax.random.normal(ks[1], (B, S, D_MODEL), jnp.float32), 'value': jax.random.normal(ks[2], (B, S, D_MODEL), jnp.float32), 'wq': jax.random.normal(ks[3], (D_MODEL, D_MODEL), jnp.float32) * s, 'bq': jnp.zeros((D_MODEL,), jnp.float32), 'wk': jax.random.normal(ks[4], (D_MODEL, D_MODEL), jnp.float32) * s, 'bk': jnp.zeros((D_MODEL,), jnp.float32), 'wv': jax.random.normal(ks[5], (D_MODEL, D_MODEL), jnp.float32) * s, 'bv': jnp.zeros((D_MODEL,), jnp.float32), 'wo': jax.random.normal(ks[6], (D_MODEL, D_MODEL), jnp.float32) * s, 'bo': jnp.zeros((D_MODEL,), jnp.float32)}
    _L0_xattn_all = _L0_xattn_setup()
    _L0_xattn_in = {k: v for k, v in _L0_xattn_all.items() if k in ('wq', 'bq', 'wk', 'bk', 'wv', 'bv', 'wo', 'bo')}
    del _L0_xattn_all

    def _L0_ffn_setup():
        import jax, jax.numpy as jnp
        import numpy as np
        D_MODEL = 128
        N_EXPERTS = 16
        TOP_K = 2
        EXPERT_DIM = 128
        SHARED_DIM = 256
        B, T = (2, 128)
        key = jax.random.key(seed)
        ks = jax.random.split(key, 7)
        std = 0.02
        return {'x': jax.random.normal(ks[0], (B, T, D_MODEL), dtype=jnp.float32), 'router_w': jax.random.normal(ks[1], (N_EXPERTS, D_MODEL), dtype=jnp.float32) * std, 'gate_up_w': jax.random.normal(ks[2], (N_EXPERTS, D_MODEL, 2 * EXPERT_DIM), dtype=jnp.float32) * std, 'down_w': jax.random.normal(ks[3], (N_EXPERTS, EXPERT_DIM, D_MODEL), dtype=jnp.float32) * std, 'shared_gate_w': jax.random.normal(ks[4], (SHARED_DIM, D_MODEL), dtype=jnp.float32) * std, 'shared_up_w': jax.random.normal(ks[5], (SHARED_DIM, D_MODEL), dtype=jnp.float32) * std, 'shared_down_w': jax.random.normal(ks[6], (D_MODEL, SHARED_DIM), dtype=jnp.float32) * std}
    _L0_ffn_all = _L0_ffn_setup()
    _L0_ffn_in = {k: v for k, v in _L0_ffn_all.items() if k in ('router_w', 'gate_up_w', 'down_w', 'shared_gate_w', 'shared_up_w', 'shared_down_w')}
    del _L0_ffn_all
    return {'x': x, 'ctx_1024': ctx_1024, 'L0_attn_sink_bias': _L0_attn_in['sink_bias'], 'L0_attn_Wq': _L0_attn_in['Wq'], 'L0_attn_bq': _L0_attn_in['bq'], 'L0_attn_Wk': _L0_attn_in['Wk'], 'L0_attn_bk': _L0_attn_in['bk'], 'L0_attn_Wv': _L0_attn_in['Wv'], 'L0_attn_bv': _L0_attn_in['bv'], 'L0_attn_Wo': _L0_attn_in['Wo'], 'L0_attn_bo': _L0_attn_in['bo'], 'L0_xattn_wq': _L0_xattn_in['wq'], 'L0_xattn_bq': _L0_xattn_in['bq'], 'L0_xattn_wk': _L0_xattn_in['wk'], 'L0_xattn_bk': _L0_xattn_in['bk'], 'L0_xattn_wv': _L0_xattn_in['wv'], 'L0_xattn_bv': _L0_xattn_in['bv'], 'L0_xattn_wo': _L0_xattn_in['wo'], 'L0_xattn_bo': _L0_xattn_in['bo'], 'L0_ffn_router_w': _L0_ffn_in['router_w'], 'L0_ffn_gate_up_w': _L0_ffn_in['gate_up_w'], 'L0_ffn_down_w': _L0_ffn_in['down_w'], 'L0_ffn_shared_gate_w': _L0_ffn_in['shared_gate_w'], 'L0_ffn_shared_up_w': _L0_ffn_in['shared_up_w'], 'L0_ffn_shared_down_w': _L0_ffn_in['shared_down_w']}

def reference(x, ctx_1024, L0_attn_sink_bias, L0_attn_Wq, L0_attn_bq, L0_attn_Wk, L0_attn_bk, L0_attn_Wv, L0_attn_bv, L0_attn_Wo, L0_attn_bo, L0_xattn_wq, L0_xattn_bq, L0_xattn_wk, L0_xattn_bk, L0_xattn_wv, L0_xattn_bv, L0_xattn_wo, L0_xattn_bo, L0_ffn_router_w, L0_ffn_gate_up_w, L0_ffn_down_w, L0_ffn_shared_gate_w, L0_ffn_shared_up_w, L0_ffn_shared_down_w):
    import jax
    import jax.numpy as jnp

    def _L0_attn_ref(x, sink_bias, Wq, bq, Wk, bk, Wv, bv, Wo, bo):
        import jax, jax.numpy as jnp
        import numpy as np
        B, S, D = (1, 512, 128)
        H, KV, WIN = (8, 2, 32)
        HD = D // H
        FP16_MIN = -65504.0
        b, s, d = x.shape
        q = (x @ Wq.T + bq).reshape(b, s, H, HD).transpose(0, 2, 1, 3)
        k = (x @ Wk.T + bk).reshape(b, s, KV, HD).transpose(0, 2, 1, 3)
        v = (x @ Wv.T + bv).reshape(b, s, KV, HD).transpose(0, 2, 1, 3)
        k = jnp.repeat(k, H // KV, axis=1)
        v = jnp.repeat(v, H // KV, axis=1)
        scores = jnp.einsum('bhqd,bhkd->bhqk', q, k) / jnp.sqrt(jnp.float32(HD))
        i = jnp.arange(s)[:, None]
        j = jnp.arange(s)[None, :]
        mask = (j <= i) & (j > i - WIN)
        scores = jnp.where(mask, scores, FP16_MIN)
        m = jnp.maximum(scores.max(axis=-1, keepdims=True), sink_bias)
        e = jnp.exp(scores - m)
        sink = jnp.exp(sink_bias - m)
        attn = e / (e.sum(axis=-1, keepdims=True) + sink)
        out = jnp.einsum('bhqk,bhkd->bhqd', attn, v)
        out = out.transpose(0, 2, 1, 3).reshape(b, s, H * HD)
        return out @ Wo.T + bo

    def _L0_xattn_ref(query, key, value, wq, bq, wk, bk, wv, bv, wo, bo):
        import jax, jax.numpy as jnp
        import numpy as np
        D_MODEL = 128
        NHEAD = 16
        D_K = D_MODEL // NHEAD
        B, Sq, _ = query.shape
        Sk = key.shape[1]
        scale = 1.0 / np.sqrt(D_K).astype(np.float32)
        Q = (query @ wq.T + bq).reshape(B, Sq, NHEAD, D_K).transpose(0, 2, 1, 3)
        K = (key @ wk.T + bk).reshape(B, Sk, NHEAD, D_K).transpose(0, 2, 1, 3)
        V = (value @ wv.T + bv).reshape(B, Sk, NHEAD, D_K).transpose(0, 2, 1, 3)
        scores = jnp.einsum('bhqd,bhkd->bhqk', Q, K) * scale
        attn = jax.nn.softmax(scores, axis=-1)
        ctx = jnp.einsum('bhqk,bhkd->bhqd', attn, V)
        ctx = ctx.transpose(0, 2, 1, 3).reshape(B, Sq, D_MODEL)
        return ctx @ wo.T + bo

    def _L0_ffn_ref(x, router_w, gate_up_w, down_w, shared_gate_w, shared_up_w, shared_down_w):
        import jax, jax.numpy as jnp
        import numpy as np
        D_MODEL = 128
        N_EXPERTS = 16
        TOP_K = 2
        EXPERT_DIM = 128
        SHARED_DIM = 256
        B, T = (2, 128)
        Bb, Tt, C = x.shape
        N = Bb * Tt
        E = gate_up_w.shape[0]
        logits = jnp.einsum('btc,ec->bte', x, router_w)
        top_vals, top_idx = jax.lax.top_k(logits, TOP_K)
        gates = jax.nn.sigmoid(top_vals)
        xf = x.reshape(N, C)
        sel = top_idx.reshape(N, TOP_K)
        gw = gates.reshape(N, TOP_K)
        w_full = jnp.zeros((N, E), dtype=x.dtype).at[jnp.arange(N)[:, None], sel].add(gw)
        gu = jnp.einsum('nc,ech->neh', xf, gate_up_w)
        gate, up = jnp.split(gu, 2, axis=-1)
        h = jax.nn.silu(gate) * up
        out_all = jnp.einsum('neh,ehc->nec', h, down_w)
        moe = jnp.einsum('ne,nec->nc', w_full, out_all).reshape(Bb, Tt, C)
        sg = jnp.einsum('btc,sc->bts', x, shared_gate_w)
        su = jnp.einsum('btc,sc->bts', x, shared_up_w)
        shared = jnp.einsum('bts,cs->btc', jax.nn.silu(sg) * su, shared_down_w)
        return moe + shared
    x = x + _L0_attn_ref(_layernorm(x, axis=-1), L0_attn_sink_bias, L0_attn_Wq, L0_attn_bq, L0_attn_Wk, L0_attn_bk, L0_attn_Wv, L0_attn_bv, L0_attn_Wo, L0_attn_bo)
    x = x + _L0_xattn_ref(_layernorm(x, axis=-1), ctx_1024, ctx_1024, L0_xattn_wq, L0_xattn_bq, L0_xattn_wk, L0_xattn_bk, L0_xattn_wv, L0_xattn_bv, L0_xattn_wo, L0_xattn_bo)
    x = x + _L0_ffn_ref(_layernorm(x, axis=-1), L0_ffn_router_w, L0_ffn_gate_up_w, L0_ffn_down_w, L0_ffn_shared_gate_w, L0_ffn_shared_up_w, L0_ffn_shared_down_w)
    return x

_drawn_inputs = setup_inputs


def setup_inputs(seed=0):
    import zlib

    import numpy as np

    out = dict(_drawn_inputs(seed))
    spreads = {'L0_attn_bq': (0.0, 0.8),
     'L0_attn_bk': (0.0, 0.8),
     'L0_attn_bv': (0.0, 0.397),
     'L0_attn_bo': (0.0, 0.1),
     'L0_xattn_bq': (0.0, 0.375),
     'L0_xattn_bk': (0.0, 0.8),
     'L0_xattn_bv': (0.0, 0.1),
     'L0_xattn_bo': (0.0, 0.1)}
    factors = {'L0_attn_Wq': 8.0,
     'L0_attn_Wk': 8.0,
     'L0_attn_Wv': 6.113,
     'L0_ffn_router_w': 8.0,
     'L0_ffn_gate_up_w': 8.0,
     'L0_ffn_down_w': 8.0,
     'L0_ffn_shared_gate_w': 7.98,
     'L0_ffn_shared_up_w': 7.848,
     'L0_ffn_shared_down_w': 7.82}
    for name, (base, spread) in spreads.items():
        noise = np.random.default_rng([zlib.crc32(name.encode()), seed]).standard_normal(out[name].shape)
        drawn = base * np.exp(spread * noise) if base else spread * noise
        out[name] = jnp.asarray(drawn.astype(out[name].dtype))
    for name, factor in factors.items():
        out[name] = (out[name] * factor).astype(out[name].dtype)
    return out
```

```python
from contextlib import ExitStack

import numpy as np

import concourse.bass as bass
from concourse import mybir

F32 = mybir.dt.float32
F16 = mybir.dt.float16
BF16 = mybir.dt.bfloat16
U32 = mybir.dt.uint32
I32 = mybir.dt.int32
ALU = mybir.AluOpType
ACT = mybir.ActivationFunctionType
AX = mybir.AxisListType

TILES, P, D = 64, 128, 128
SK = 120
H, KV, HD = 8, 2, 16
WIN = 32
XH, XD = 16, 8
E, EH = 16, 128
SH = 256
EPS = 1e-5
FP16_MIN = -65504.0
REGION = TILES * P + P
DUMMY = E * REGION
BLOCKS = (2 * TILES * P + E * (P - 1)) // P + 1
PAIRS = BLOCKS // 2
SPARE = BLOCKS - 2 * TILES
ROWS = DUMMY + SPARE * P
RING = 4
GRING = 4

SKEW = {"ln1": -1, "self": 0, "ln2": 0, "cross": 1, "xout": 2, "ln3": 2, "ffn": 3}
FIRST_STEP, LAST_STEP = -1, TILES + 2
AHEAD = 4
EARLY = 36
LOOP_FROM, LOOP_TO = 4, TILES - 1


def constants():
    p = np.arange(P)
    band = (p[None, :] <= p[:, None]) & (p[None, :] > p[:, None] - WIN)
    small = np.zeros((P, 128), np.float32)
    small[:, 64:128] = np.arange(TILES) * P
    small[:, 38:42] = (p[:, None] % 64 // HD) == np.arange(4)
    small[:, 2:6] = (p[:, None] % 32 // XD) == np.arange(4)
    small[:, 6:22] = np.arange(E)
    small[:, 22:38] = np.arange(E) * REGION
    return {
        "c_ident": np.eye(P, dtype=np.float32),
        "c_band": np.concatenate([np.eye(P), np.where(band, 0.0, FP16_MIN)], 1).astype(np.float16),
        "c_tri": np.concatenate([p[:, None] < p[None, :], np.ones((P, P))], 1).astype(np.float16),
        "c_small": small,
        "c_blocks": np.arange(BLOCKS, dtype=np.float32)[None, :],
    }


def decoder_program(nc, A, out):
    sent = nc.dram_tensor("sent_rows", [ROWS, D], F32, kind="Internal").ap()
    made = nc.dram_tensor("made_rows", [BLOCKS * P, D], F32, kind="Internal").ap()

    with ExitStack() as ctx:
        def sb(name, shape, dt=F32):
            return ctx.enter_context(nc.sbuf_tensor(name, shape, dt))

        def sem(name):
            return ctx.enter_context(nc.semaphore(name))

        X = sb("X", [P, TILES, D])
        ctx_now = sb("ctx_now", [SK, D])
        w_sq = sb("w_sq", [P, P]); w_sk = sb("w_sk", [P, P]); w_sv = sb("w_sv", [P, KV * HD]); w_so = sb("w_so", [P, P])
        w_xq = sb("w_xq", [P, P]); w_xk = sb("w_xk", [P, P]); w_xv = sb("w_xv", [P, P]); w_xo = sb("w_xo", [P, P])
        w_router = sb("w_router", [P, E])
        w_shared = sb("w_shared", [P, 2 * SH])
        w_sdown = sb("w_sdown", [P, 2, D])
        w_up = sb("w_up", [P, E, 2 * EH])
        w_down = sb("w_down", [P, E, D])
        b_cols = sb("b_cols", [P, 6])
        b_q, b_k, bx_q, bx_k, sink, b_q4 = (b_cols[:, n:n + 1] for n in range(6))
        b_v = sb("b_v", [P, KV * HD]); b_o = sb("b_o", [P, D]); bx_v = sb("bx_v", [P, D]); bx_o = sb("bx_o", [P, D])
        ident = sb("ident", [P, P]); band = sb("band", [P, 2, P], F16); tri = sb("tri", [P, 2, P], F16)
        small = sb("small", [P, 128])
        half_s, half_x, iota_e, base0, steps = small[:, 38:42], small[:, 2:6], small[:, 6:22], small[:, 22:38], small[:, 64:128]
        minus_half = sb("minus_half", [P, 1])
        stats = {n: sb(f"stats_{n}", [P, 6]) for n in ("ln1", "ln2", "ln3")}
        mv = {n: sb(f"mv_{n}", [P, 2]) for n in ("ln1", "ln2", "ln3")}
        var = {n: sb(f"var_{n}", [P, 1]) for n in ("ln1", "ln2", "ln3")}
        rstd = {n: sb(f"rstd_{n}", [P, 1]) for n in ("ln1", "ln2", "ln3")}
        xn = {n: sb(f"xn_{n}", [P, D]) for n in ("ln1", "ln2", "ln3")}
        xT_s = sb("xT_s", [P, P]); q_s = sb("q_s", [P, P]); k_s = sb("k_s", [P, 4, P]); v_s = sb("v_s", [P, KV, HD + 1])
        max_s = sb("max_s", [P, H]); esink = sb("esink", [P, H]); z_s = sb("z_s", [P, H, P]); e_s = sb("e_s", [P, H, P])
        den_s = sb("den_s", [P, H]); o_s = sb("o_s", [P, H, HD]); oT_s = sb("oT_s", [P, P]); xb_s = sb("xb_s", [P, D])
        xcT = sb("xcT", [P, P + SK]); q_x = sb("q_x", [P, P]); k_x = sb("k_x", [P, 4, SK]); v_x = sb("v_x", [P, XH, XD + 1])
        max_x = sb("max_x", [P, XH]); z_x = sb("z_x", [P, XH, SK]); e_x = sb("e_x", [P, XH, P])
        den_x = sb("den_x", [P, XH]); o_x = sb("o_x", [P, XH, XD]); oT_x = sb("oT_x", [P, P]); xb_x = sb("xb_x", [P, D])
        xT_f = sb("xT_f", [P, P]); th_f = sb("th_f", [P, SH]); g_f = sb("g_f", [P, SH]); h_f = sb("h_f", [P, SH]); hT_f = sb("hT_f", [P, 2, P])
        logit = sb("logit", [P, E]); top = sb("top", [P, 8]); top_i = sb("top_i", [P, 8], U32); top_f = sb("top_f", [P, 2])
        hot = sb("hot", [P, 2, E]); hots = sb("hots", [P, E], F16); base = sb("base", [P, E]); place = sb("place", [P, E])
        picked = sb("picked", [P, 2, E]); row_f = sb("row_f", [P, 2]); row_i = sb("row_i", [P, 2], U32)
        ROW = sb("ROW", [P, TILES, 2])
        GATE = sb("GATE", [P, TILES, 2])
        blocks = sb("blocks", [1, BLOCKS]); zero = sb("zero", [P, P])
        count = sb("count", [P, E]); full = sb("full", [P, E, TILES]); n_blk = sb("n_blk", [P, E]); ends = sb("ends", [P, E])
        jump = sb("jump", [P, E]); passed_e = sb("passed_e", [P, 2 * TILES, E - 1]); shift = sb("shift", [P, 2 * TILES]); MADE = sb("MADE", [P, TILES, 2], U32)
        past = sb("past", [1, BLOCKS, E]); of = sb("of", [1, BLOCKS]); at = sb("at", [1, BLOCKS]); live = sb("live", [1, BLOCKS])
        off_f = sb("off_f", [1, 3, BLOCKS]); table = sb("table", [1, 3, BLOCKS], I32)
        tail = sb("tail", [1, E], I32)
        rows_in = sb("rows_in", [P, RING, 2, D]); xT_e = sb("xT_e", [P, 2, P]); th_e = sb("th_e", [P, 2, EH])
        g_e = sb("g_e", [P, 2, EH]); h_e = sb("h_e", [P, 2, EH]); hT_e = sb("hT_e", [P, 2, P]); rows_out = sb("rows_out", [P, RING, 2, D])
        idx = sb("idx", [P, GRING, 2], U32); back = sb("back", [P, GRING, 2, D]); summed = sb("summed", [P, GRING, D])

        PS = ctx.enter_context(nc.psum_tensor("PS", [P, 8, 512], F32))
        SC = [PS[:, 0:2, :], PS[:, 2:4, :]]
        TR = [PS[:, 4, :], PS[:, 5, :]]
        M0, M1 = PS[:, 6, :], PS[:, 7, :]

        names = """w_early w_late s_const b_ready x_in ctx_in zeroed
            ln1_stats ln1_mv ln1_var ln1_rstd ln1_x ln2_stats ln2_mv ln2_var ln2_rstd ln2_x ln3_stats ln3_mv ln3_var ln3_rstd ln3_x
            s_xT_ps s_xT s_q_ps s_q s_kv_ps s_k s_v s_sc s_rowmax s_max s_z s_esink s_tr s_e s_pv s_den s_rden s_o s_oT_ps s_oT s_out_ps s_xb s_done
            x_T_ps x_T x_q_ps x_q x_kv_ps x_k x_v x_sc x_max x_z x_tr x_e x_pv x_rden x_o x_oT_ps x_oT x_out_ps x_xb x_done
            f_xT_ps f_xT f_lg_ps f_logit f_top f_topi f_topf f_hot f_hots f_gate f_gu_ps f_th f_g f_h f_rank_ps f_place f_base f_pick f_rowf f_row f_rowlog f_sent f_hT_ps f_hT f_dn_ps f_done
            t_step t_made t_table t_tail w_half e_xT_ps e_xT e_gu_ps e_th e_g e_h e_hT_ps e_hT e_y_ps e_y
            passed g_idx g_gate g_sum g_done g_out""".split()
        S = {n: sem(n) for n in names}
        for u in range(RING):
            S[f"e_in{u}"] = sem(f"e_in{u}")
            S[f"e_out{u}"] = sem(f"e_out{u}")
        for u in range(GRING):
            S[f"g_back{u}"] = sem(f"g_back{u}")

        def at_block(row, j, a):
            return table[0:1, row, 2 * j + a:2 * j + a + 1] if isinstance(j, int) else table[0:1, row, bass.ds(j * 2 + a, 1)]

        def steps_of(eng, body):
            for i in range(FIRST_STEP, LOOP_FROM):
                body(i)
            with eng.Fori(LOOP_FROM, LOOP_TO) as i:
                body(i)
            for i in range(LOOP_TO, LAST_STEP + 1):
                body(i)

        def runs(stage, i):
            return not isinstance(i, int) or 0 <= i - SKEW[stage] < TILES

        def done(stage, i):
            n = i - SKEW[stage] + 1
            return max(0, min(TILES, n)) if isinstance(i, int) else n

        def before(stage, i):
            return done(stage, i - 1)

        def wait(eng, name, n, per=1):
            if isinstance(n, int) and n <= 0:
                return
            eng.wait_ge(S[name], n * per if per != 1 else n)

        def tile(buf, stage, i):
            t = i - SKEW[stage]
            return buf[:, t, :] if isinstance(t, int) else buf[:, bass.ds(t, 1), :].rearrange("p a d -> p (a d)")

        def passed(eng):
            eng.sem_inc(S["passed"], 1)

        def met(eng):
            eng.wait_ge(S["s_const"], 5)

        def wait_part(eng, name, n, parts, c):
            eng.wait_ge(S[name], n * parts - (parts - 1 - c))

        def pairs_of(eng, body):
            for j in range(2 * RING):
                body(j, j % RING)
            with eng.Fori(2, PAIRS // RING) as r:
                for u in range(RING):
                    body(r * RING + u, u)
            for j in range(PAIRS, PAIRS + 3):
                body(j, j % RING)

        block = ctx.enter_context(nc.Block())

        @block.sync
        def _(sp):
            n = 0
            for dst, src in ((ident, A["c_ident"]), (w_sq, A["wq"]), (small, A["c_small"]),
                             (w_sv, A["wv"]), (band, A["c_band"].rearrange("p (a b) -> p a b", a=2)), (w_so, A["wo"]),
                             (w_xq, A["xwq"]), (w_xk, A["xwk"]), (w_xv, A["xwv"]), (w_xo, A["xwo"]),
                             (w_router, A["router"]), (tri, A["c_tri"].rearrange("p (a b) -> p a b", a=2))):
                sp.dma_start(dst[:], src).then_inc(S["w_early"], 16)
                n += 1
            for h in range(H):
                kv = h // (H // KV)
                sp.dma_start(w_sk[:, h * HD:(h + 1) * HD], A["wk"][:, kv * HD:(kv + 1) * HD]).then_inc(S["w_early"], 16)
                sp.dma_start(b_k[h * HD:(h + 1) * HD, :], A["bk"][kv * HD:(kv + 1) * HD].rearrange("(p a) -> p a", a=1)).then_inc(S["w_early"], 16)
                n += 2
            for dst, src in ((b_q, A["bq"]), (bx_q, A["xbq"]), (bx_k, A["xbk"])):
                sp.dma_start(dst, src.rearrange("(p a) -> p a", a=1)).then_inc(S["w_early"], 16)
                n += 1
            for dst, src in ((b_v, A["bv"]), (b_o, A["bo"]), (bx_v, A["xbv"]), (bx_o, A["xbo"]), (sink, A["sink"])):
                sp.dma_start(dst[:], src.rearrange("(a n) -> a n", a=1).to_broadcast([P, src.shape[0]])).then_inc(S["w_early"], 16)
                n += 1
            assert n == EARLY
            for dst, src in ((w_shared[:, 0:SH], A["shared_gate"]), (w_shared[:, SH:], A["shared_up"]),
                             (w_sdown, A["shared_down"].rearrange("(c p) d -> p c d", p=P))):
                sp.dma_start(dst[:], src).then_inc(S["w_early"], 16)
            for t in range(AHEAD):
                sp.dma_start(X[:, t, :], A["x"][t, :, :]).then_inc(S["x_in"], 16)
                sp.wait_ge(S["x_in"], t * 16 + 16)
            for dst, src in ((w_up, A["gate_up"].rearrange("e p n -> p e n")), (w_down, A["down"].rearrange("e p n -> p e n")),
                             (blocks, A["c_blocks"])):
                sp.dma_start(dst[:], src).then_inc(S["w_late"], 16)
            sp.dma_start(ctx_now[:], A["ctx"][0, :, :]).then_inc(S["ctx_in"], 16)
            with sp.Fori(1, TILES - AHEAD + 1) as t:
                sp.dma_start(X[:, bass.ds(t + (AHEAD - 1), 1), :], A["x"][bass.ds(t + (AHEAD - 1), 1), :, :].rearrange("a p d -> p a d")).then_inc(S["x_in"], 16)
                sp.wait_ge(S["x_T_ps"], t)
                sp.dma_start(ctx_now[:], A["ctx"][bass.ds(t, 1), :, :].rearrange("a p d -> p (a d)")).then_inc(S["ctx_in"], 16)
                sp.wait_ge(S["x_in"], t * 16 + AHEAD * 16)
                passed(sp)
            for t in range(TILES - AHEAD + 1, TILES):
                sp.wait_ge(S["x_T_ps"], t)
                sp.dma_start(ctx_now[:], A["ctx"][t, :, :]).then_inc(S["ctx_in"], 16)
            sp.wait_ge(S["s_const"], 5)
            for b in range(SPARE):
                sp.dma_start(sent[DUMMY + b * P:DUMMY + (b + 1) * P, :], zero[:]).then_inc(S["zeroed"], 16)
            sp.wait_ge(S["t_tail"], 1)
            for e in range(E):
                r = sp.value_load(tail[0:1, e:e + 1], min_val=0, max_val=DUMMY - P)
                sp.dma_start(sent[bass.ds(r, P), :], zero[:]).then_inc(S["zeroed"], 16)
            sp.wait_ge(S["zeroed"], 16 * (SPARE + E))
            sp.wait_ge(S["f_sent"], 32 * TILES)
            sp.wait_ge(S["t_table"], 1)

            def load(j, u):
                for a in range(2):
                    r = sp.value_load(at_block(0, j, a), min_val=0, max_val=ROWS - P)
                    sp.dma_start(rows_in[:, u, a, :], sent[bass.ds(r, P), :]).then_inc(S[f"e_in{u}"], 16)

            for j in range(RING):
                load(j, j)
            with sp.Fori(1, PAIRS // RING) as r:
                for u in range(RING):
                    sp.wait_ge(S["e_xT_ps"], r * RING + (u + 1 - RING))
                    load(r * RING + u, u)
            with sp.Fori(0, TILES) as t:
                sp.wait_ge(S["g_done"], t + 1)
                sp.dma_start(out[bass.ds(t, 1), :, :].rearrange("a p d -> p a d"), X[:, bass.ds(t, 1), :]).then_inc(S["g_out"], 16)
            sp.wait_ge(S["g_out"], 16 * TILES)


        @block.tensor
        def _(pe):
            pe.wait_ge(S["w_early"], 16 * (EARLY + 3))

            pe.wait_ge(S["w_half"], 1)

            def m0_free(i):
                wait(pe, "x_o", before("cross", i))
                if isinstance(i, int):
                    wait(pe, "s_v", before("self", i))
                    wait(pe, "f_done", before("ffn", i))

            def m1_free(i):
                wait(pe, "s_done", before("self", i))
                if isinstance(i, int):
                    wait(pe, "x_v", before("cross", i))
                    wait(pe, "x_done", before("xout", i))
                    wait(pe, "f_base", before("ffn", i))

            def step(i):
                if runs("self", i):
                    wait(pe, "ln1_x", done("self", i))
                    m0_free(i)
                    pe.transpose(M0[:, 0:P], xn["ln1"][:], ident[:]).then_inc(S["s_xT_ps"], 1)
                if runs("xout", i):
                    wait(pe, "x_o", done("xout", i))
                    m1_free(i)
                    pe.transpose(M1[:, 0:P], o_x[:].rearrange("p h d -> p (h d)"), ident[:]).then_inc(S["x_oT_ps"], 1)
                if runs("ffn", i):
                    wait(pe, "ln3_x", done("ffn", i))
                    m0_free(i)
                    wait(pe, "s_xT", done("self", i))
                    pe.transpose(M0[:, 0:P], xn["ln3"][:], ident[:]).then_inc(S["f_xT_ps"], 1)
                if runs("self", i):
                    wait(pe, "s_xT", done("self", i))
                    wait(pe, "x_oT", done("xout", i))
                    m1_free(i)
                    pe.matmul(M1[:, 0:P], w_sq[:], xT_s[:], start=True, stop=True).then_inc(S["s_q_ps"], 1)
                    wait(pe, "f_xT", done("ffn", i))
                    pe.matmul(M0[:, 0:P], w_sk[:], xT_s[:], start=True, stop=True)
                    pe.matmul(M0[:, P:P + KV * HD], xT_s[:], w_sv[:], start=True, stop=True).then_inc(S["s_kv_ps"], 1)
                if runs("xout", i):
                    wait(pe, "x_oT", done("xout", i))
                    wait(pe, "s_q", done("self", i))
                    pe.matmul(M1[:, 0:D], oT_x[:], w_xo[:], start=True, stop=True).then_inc(S["x_out_ps"], 1)
                if runs("ffn", i):
                    wait(pe, "f_xT", done("ffn", i))
                    wait(pe, "s_v", done("self", i))
                    wait(pe, "s_k", done("self", i))
                    pe.matmul(M0[:, 0:E], xT_f[:], w_router[:], start=True, stop=True).then_inc(S["f_lg_ps"], 1)
                if runs("self", i):
                    wait(pe, "s_q", done("self", i))
                    wait(pe, "s_k", done("self", i))
                    wait(pe, "x_z", before("cross", i), 2)
                    for b in range(2):
                        pe.matmul(SC[0][:, b, :].rearrange("p (h k) -> p h k", k=P), band[:, 0, :],
                                  band[:, 1:2, :].to_broadcast([P, 4, P]), start=True, stop=False)
                        mm = pe.matmul(SC[0][:, b, :], q_s[64 * b:64 * b + 64, :], k_s[64 * b:64 * b + 64, :, :].rearrange("p h k -> p (h k)"),
                                       start=False, stop=True, tile_position=(64 * b, 0))
                    mm.then_inc(S["s_sc"], 1)
                if runs("cross", i):
                    wait(pe, "ln2_x", done("cross", i))
                    wait(pe, "ctx_in", done("cross", i), 16)
                    wait(pe, "x_done", done("xout", i))
                    wait(pe, "s_q", done("self", i))
                    m1_free(i)
                    pe.transpose(M1[:, 0:P], xn["ln2"][:], ident[:])
                    pe.transpose(M1[:, P:P + SK], ctx_now[:], ident[0:SK, 0:SK]).then_inc(S["x_T_ps"], 1)
                if runs("ffn", i):
                    wait(pe, "f_logit", done("ffn", i))
                    pe.matmul(M0[:, :], xT_f[:], w_shared[:], start=True, stop=True).then_inc(S["f_gu_ps"], 1)
                if runs("cross", i):
                    wait(pe, "x_T", done("cross", i))
                    pe.matmul(M1[:, 0:P], w_xq[:], xcT[:, 0:P], start=True, stop=True).then_inc(S["x_q_ps"], 1)
                    wait(pe, "x_q", done("cross", i))
                    pe.matmul(M1[:, 0:SK], w_xk[:], xcT[:, P:P + SK], start=True, stop=True)
                    pe.matmul(M1[0:SK, P:2 * P], xcT[:, P:P + SK], w_xv[:], start=True, stop=True).then_inc(S["x_kv_ps"], 1)
                if runs("ffn", i):
                    wait(pe, "f_hots", done("ffn", i))
                    wait(pe, "x_v", done("cross", i))
                    m1_free(i)
                    pe.matmul(M1[:, 0:E], tri[:, 0, :], hots[:], start=True, stop=True)
                    pe.matmul(M1[:, E:2 * E], tri[:, 1, :], hots[:], start=True, stop=True).then_inc(S["f_rank_ps"], 1)
                if runs("self", i):
                    wait(pe, "s_z", done("self", i))
                    for c in range(2):
                        wait(pe, "x_e", before("cross", i), 4)
                        wait(pe, "s_e", before("self", i), 2)
                        for j in range(4):
                            mm = pe.transpose(TR[c][:, j * P:(j + 1) * P], z_s[:, 4 * c + j, :], ident[:])
                        mm.then_inc(S["s_tr"], 1)
                if runs("cross", i):
                    wait(pe, "x_q", done("cross", i))
                    wait(pe, "x_k", done("cross", i))
                    for half in range(2):
                        if half == 0:
                            wait(pe, "x_z", before("cross", i), 2)
                        else:
                            wait(pe, "s_z", done("self", i))
                            wait(pe, "x_z", before("cross", i), 2)
                        for b in range(2):
                            g = 2 * half + b
                            mm = pe.matmul(SC[1 - half][:, b, 0:4 * SK], q_x[32 * g:32 * g + 32, :],
                                           k_x[32 * g:32 * g + 32, :, :].rearrange("p h k -> p (h k)"),
                                           start=True, stop=True, tile_position=(32 * g, 0))
                        mm.then_inc(S["x_sc"], 1)
                if runs("self", i):
                    wait(pe, "s_e", done("self", i), 2)
                    wait(pe, "s_v", done("self", i))
                    wait(pe, "f_base", done("ffn", i))
                    wait(pe, "f_place", done("ffn", i))
                    wait(pe, "x_v", done("cross", i))
                    wait(pe, "x_k", done("cross", i))
                    for h in range(H):
                        mm = pe.matmul(M1[:, h * (HD + 1):(h + 1) * (HD + 1)], e_s[:, h, :], v_s[:, h // (H // KV), :],
                                       start=True, stop=True)
                    mm.then_inc(S["s_pv"], 1)
                if runs("ffn", i):
                    wait(pe, "f_h", done("ffn", i))
                    for c in range(2):
                        mm = pe.transpose(M0[:, c * P:(c + 1) * P], h_f[:, c * P:(c + 1) * P], ident[:])
                    mm.then_inc(S["f_hT_ps"], 1)

                def cross_transposes(c):
                    if c < 2:
                        wait(pe, "s_e", done("self", i), 2)
                        wait(pe, "x_e", before("cross", i), 4)
                    else:
                        pe.wait_ge(S["x_e"], nx * 4 - 4 + (c - 1))
                    for j in range(4):
                        mm = pe.transpose(TR[c % 2][0:SK, j * P:(j + 1) * P], z_x[:, 4 * c + j, :], ident[:])
                    mm.then_inc(S["x_tr"], 1)

                nx = done("cross", i)
                if runs("cross", i):
                    pe.wait_ge(S["x_z"], nx * 2 - 1)
                    cross_transposes(0)
                    cross_transposes(1)
                if runs("self", i):
                    wait(pe, "s_o", done("self", i))
                    pe.transpose(M1[:, 0:P], o_s[:].rearrange("p h d -> p (h d)"), ident[:]).then_inc(S["s_oT_ps"], 1)
                if runs("ffn", i):
                    wait(pe, "f_hT", done("ffn", i))
                    pe.matmul(M0[:, 0:D], hT_f[:, 0, :], w_sdown[:, 0, :], start=True, stop=False)
                    pe.matmul(M0[:, 0:D], hT_f[:, 1, :], w_sdown[:, 1, :], start=False, stop=True).then_inc(S["f_dn_ps"], 1)
                if runs("self", i):
                    wait(pe, "s_oT", done("self", i))
                    pe.matmul(M1[:, 0:D], oT_s[:], w_so[:], start=True, stop=True).then_inc(S["s_out_ps"], 1)
                if runs("cross", i):
                    pe.wait_ge(S["x_z"], nx * 2)
                    cross_transposes(2)
                    cross_transposes(3)
                    pe.wait_ge(S["x_e"], nx * 4)
                    wait(pe, "x_v", nx)
                    wait(pe, "f_done", done("ffn", i))
                    wait(pe, "s_v", done("self", i))
                    wait(pe, "s_k", done("self", i))
                    wait(pe, "x_o", before("cross", i))
                    for h in range(XH):
                        mm = pe.matmul(M0[:, h * (XD + 1):(h + 1) * (XD + 1)], e_x[0:SK, h, :], v_x[0:SK, h, :],
                                       start=True, stop=True)
                    mm.then_inc(S["x_pv"], 1)

            steps_of(pe, step)

            XT, GU, HT, Y = (PS[:, b, :] for b in range(4))
            pe.wait_ge(S["x_o"], TILES)
            pe.wait_ge(S["f_done"], TILES)
            pe.wait_ge(S["w_late"], 16 * 3)
            pe.wait_ge(S["w_half"], 2)
            pe.wait_ge(S["t_table"], 1)

            def pair(j, u):
                static = isinstance(j, int)
                if not static or 0 <= j - 3 < PAIRS:
                    pe.wait_ge(S["e_hT"], j - 2)
                    if not static or j - 3 > 0:
                        pe.wait_ge(S["e_y"], j - 3)
                    for a in range(2):
                        o = pe.value_load(at_block(2, j - 3, a), min_val=0, max_val=(E - 1) * D)
                        mm = pe.matmul(Y[:, a * D:(a + 1) * D], hT_e[:, a, :], w_down[:].rearrange("p e n -> p (e n)")[:, bass.ds(o, D)],
                                       start=True, stop=True)
                    mm.then_inc(S["e_y_ps"], 1)
                if not static or 0 <= j - 2 < PAIRS:
                    pe.wait_ge(S["e_h"], j - 1)
                    if not static or j - 2 > 0:
                        pe.wait_ge(S["e_hT"], j - 2)
                    for a in range(2):
                        mm = pe.transpose(HT[:, a * P:(a + 1) * P], h_e[:, a, :], ident[:])
                    mm.then_inc(S["e_hT_ps"], 1)
                if not static or 0 <= j - 1 < PAIRS:
                    pe.wait_ge(S["e_xT"], j)
                    if not static or j - 1 > 0:
                        pe.wait_ge(S["e_h"], j - 1)
                    for a in range(2):
                        o = pe.value_load(at_block(1, j - 1, a), min_val=0, max_val=(E - 1) * 2 * EH)
                        mm = pe.matmul(GU[:, a * 2 * EH:(a + 1) * 2 * EH], xT_e[:, a, :],
                                       w_up[:].rearrange("p e n -> p (e n)")[:, bass.ds(o, 2 * EH)], start=True, stop=True)
                    mm.then_inc(S["e_gu_ps"], 1)
                if not static or 0 <= j < PAIRS:
                    if static:
                        pe.wait_ge(S[f"e_in{u}"], 32 * (j // RING + 1))
                        if j > 0:
                            pe.wait_ge(S["e_xT"], j)
                    else:
                        pe.wait_ge(S[f"e_in{u}"], (j - u) * (32 // RING) + 32)
                        pe.wait_ge(S["e_xT"], j)
                    for a in range(2):
                        mm = pe.transpose(XT[:, a * P:(a + 1) * P], rows_in[:, u, a, :], ident[:])
                    mm.then_inc(S["e_xT_ps"], 1)

            pairs_of(pe, pair)

        @block.scalar
        def _(act):
            act.wait_ge(S["w_early"], 16 * (EARLY + 3))
            nc.scalar.mul(b_q4, b_q, 1.0 / HD ** 0.5).then_inc(S["b_ready"], 1)
            act.wait_ge(S["b_ready"], 1)

            def step(i):
                if runs("self", i):
                    wait(act, "s_xT_ps", done("self", i))
                    wait(act, "s_kv_ps", before("self", i))
                    nc.scalar.copy(xT_s[:], M0[:, 0:P]).then_inc(S["s_xT"], 1)
                if runs("xout", i):
                    wait(act, "x_oT_ps", done("xout", i))
                    wait(act, "x_out_ps", before("xout", i))
                    nc.scalar.copy(oT_x[:], M1[:, 0:P]).then_inc(S["x_oT"], 1)
                if runs("ffn", i):
                    wait(act, "f_xT_ps", done("ffn", i))
                    wait(act, "f_gu_ps", before("ffn", i))
                    nc.scalar.copy(xT_f[:], M0[:, 0:P]).then_inc(S["f_xT"], 1)
                if runs("self", i):
                    wait(act, "s_q_ps", done("self", i))
                    wait(act, "s_sc", before("self", i))
                    nc.scalar.activation(q_s[:], M1[:, 0:P], ACT.Identity, bias=b_q4, scale=1.0 / HD ** 0.5).then_inc(S["s_q"], 1)
                if runs("cross", i):
                    wait(act, "x_T_ps", done("cross", i))
                    wait(act, "x_kv_ps", before("cross", i))
                    nc.scalar.copy(xcT[:], M1[:, 0:P + SK]).then_inc(S["x_T"], 1)
                if runs("ffn", i):
                    wait(act, "f_gu_ps", done("ffn", i))
                    wait(act, "f_g", before("ffn", i))
                    nc.scalar.activation(th_f[:], M0[:, 0:SH], ACT.Tanh, scale=0.5).then_inc(S["f_th"], 1)
                if runs("cross", i):
                    wait(act, "x_q_ps", done("cross", i))
                    wait(act, "x_sc", before("cross", i), 2)
                    nc.scalar.activation(q_x[:], M1[:, 0:P], ACT.Identity, bias=bx_q).then_inc(S["x_q"], 1)
                if runs("ffn", i):
                    wait(act, "f_top", done("ffn", i))
                    nc.scalar.activation(tile(GATE, "ffn", i), top[:, 0:2], ACT.Tanh, scale=0.5).then_inc(S["f_gate"], 1)
                if runs("self", i):
                    wait(act, "s_max", done("self", i))
                    wait(act, "s_den", before("self", i))
                    nc.scalar.activation(esink[:], max_s[:], ACT.Exp, bias=sink, scale=-1.0).then_inc(S["s_esink"], 1)
                    wait(act, "s_pv", before("self", i))
                    for c in range(2):
                        wait_part(act, "s_tr", done("self", i), 2, c)
                        nc.scalar.activation(e_s[:, 4 * c:4 * c + 4, :], TR[c].rearrange("p (h q) -> p h q", q=P), ACT.Exp).then_inc(S["s_e"], 1)
                if runs("ffn", i):
                    wait(act, "f_hT_ps", done("ffn", i))
                    wait(act, "f_dn_ps", before("ffn", i))
                    nc.scalar.copy(hT_f[:].rearrange("p c q -> p (c q)"), M0[:, 0:2 * P]).then_inc(S["f_hT"], 1)

                def cross_exp(c):
                    wait_part(act, "x_tr", done("cross", i), 4, c)
                    nc.scalar.activation(e_x[0:SK, 4 * c:4 * c + 4, :], TR[c % 2][0:SK, :].rearrange("p (h q) -> p h q", q=P),
                                         ACT.Exp, scale=1.0 / XD ** 0.5).then_inc(S["x_e"], 1)

                if runs("cross", i):
                    wait(act, "x_pv", before("cross", i))
                    cross_exp(0)
                    cross_exp(1)
                if runs("self", i):
                    wait(act, "s_oT_ps", done("self", i))
                    wait(act, "s_out_ps", before("self", i))
                    nc.scalar.copy(oT_s[:], M1[:, 0:P]).then_inc(S["s_oT"], 1)
                if runs("cross", i):
                    cross_exp(2)
                    cross_exp(3)

            steps_of(act, step)

            XT, GU, HT, Y = (PS[:, b, :] for b in range(4))

            def pair(j, u):
                static = isinstance(j, int)
                if not static or 0 <= j - 2 < PAIRS:
                    pe_n = j - 1
                    act.wait_ge(S["e_hT_ps"], pe_n)
                    if not static or j - 2 > 0:
                        act.wait_ge(S["e_y_ps"], j - 2)
                    nc.scalar.copy(hT_e[:].rearrange("p a q -> p (a q)"), HT[:, 0:2 * P]).then_inc(S["e_hT"], 1)
                if not static or 0 <= j - 1 < PAIRS:
                    act.wait_ge(S["e_gu_ps"], j)
                    if not static or j - 1 > 0:
                        act.wait_ge(S["e_g"], j - 1)
                    nc.scalar.activation(th_e[:], GU.rearrange("p (a n) -> p a n", a=2)[:, :, 0:EH], ACT.Tanh, scale=0.5).then_inc(S["e_th"], 1)
                if not static or 0 <= j < PAIRS:
                    act.wait_ge(S["e_xT_ps"], j + 1)
                    if not static or j > 0:
                        act.wait_ge(S["e_gu_ps"], j)
                    nc.scalar.copy(xT_e[:].rearrange("p a q -> p (a q)"), XT[:, 0:2 * P]).then_inc(S["e_xT"], 1)

            pairs_of(act, pair)

        @block.vector
        def _(dve):
            nc.vector.memset(minus_half[:], -0.5).then_inc(S["s_const"], 1)
            nc.vector.memset(zero[:], 0.0).then_inc(S["s_const"], 1)
            nc.vector.memset(v_s[:], 1.0).then_inc(S["s_const"], 1)
            nc.vector.memset(v_x[:], 1.0).then_inc(S["s_const"], 1)
            dve.wait_ge(S["w_early"], 16 * (EARLY + 3))
            nc.vector.tensor_copy(base[:], base0).then_inc(S["s_const"], 1)
            dve.wait_ge(S["s_const"], 5)

            def layer_norm(ln, i):
                n = done(ln, i)
                nc.vector.bn_stats(stats[ln][:], tile(X, ln, i)).then_inc(S[ln + "_stats"], 1)
                met(dve)
                wait(dve, ln + "_stats", n)
                wait(dve, ln + "_var", before(ln, i))
                nc.vector.bn_aggr(mv[ln][:], stats[ln][:]).then_inc(S[ln + "_mv"], 1)

            def normed(ln, i, waits):
                n = done(ln, i)
                wait(dve, ln + "_rstd", n)
                for name, count, per in waits:
                    wait(dve, name, count, per)
                nc.vector.tensor_scalar(xn[ln][:], tile(X, ln, i), mv[ln][:, 0:1], rstd[ln][:], ALU.subtract, ALU.mult).then_inc(S[ln + "_x"], 1)

            def step(i):
                ns, nx, nf = done("self", i), done("cross", i), done("ffn", i)
                if runs("self", i):
                    wait(dve, "s_kv_ps", ns)
                    wait(dve, "s_sc", before("self", i))
                    nc.vector.scalar_tensor_tensor(out=k_s[:], in0=M0[:, 0:P].rearrange("p (a k) -> p a k", a=1).to_broadcast([P, 4, P]), scalar=b_k,
                                                   in1=half_s.rearrange("p (h a) -> p h a", a=1).to_broadcast([P, 4, P]),
                                                   op0=ALU.add, op1=ALU.mult).then_inc(S["s_k"], 1)
                    wait(dve, "s_pv", before("self", i))
                    nc.vector.tensor_tensor(v_s[:, :, 0:HD], M0[:, P:P + KV * HD].rearrange("p (h d) -> p h d", h=KV),
                                            b_v[:].rearrange("p (h d) -> p h d", h=KV), ALU.add).then_inc(S["s_v"], 1)
                if runs("xout", i):
                    wait(dve, "x_out_ps", done("xout", i))
                    wait(dve, "x_xb", done("xout", i))
                    nc.vector.tensor_tensor(tile(X, "xout", i), M1[:, 0:D], xb_x[:], ALU.add).then_inc(S["x_done"], 1)
                if runs("ffn", i):
                    wait(dve, "f_lg_ps", nf)
                    wait(dve, "f_topi", before("ffn", i))
                    nc.vector.tensor_copy(logit[:], M0[:, 0:E]).then_inc(S["f_logit"], 1)
                    met(dve)
                    wait(dve, "f_logit", nf)
                    wait(dve, "f_gate", before("ffn", i))
                    nc.vector.max(top[:], logit[:]).then_inc(S["f_top"], 1)
                    met(dve)
                    wait(dve, "f_top", nf)
                    nc.vector.max_index(top_i[:], top[:], logit[:]).then_inc(S["f_topi"], 1)
                    wait(dve, "f_topi", nf)
                    nc.vector.tensor_copy(top_f[:], top_i[:, 0:2]).then_inc(S["f_topf"], 1)
                    wait(dve, "f_topf", nf)
                    nc.vector.tensor_tensor(hot[:], iota_e.rearrange("p (a e) -> p a e", a=1).to_broadcast([P, 2, E]),
                                            top_f[:].rearrange("p (s a) -> p s a", a=1).to_broadcast([P, 2, E]), ALU.is_equal).then_inc(S["f_hot"], 1)
                    wait(dve, "f_hot", nf)
                    wait(dve, "f_rank_ps", before("ffn", i))
                    nc.vector.tensor_tensor(hots[:], hot[:, 0, :], hot[:, 1, :], ALU.add).then_inc(S["f_hots"], 1)
                if runs("self", i):
                    wait(dve, "s_sc", ns)
                    wait(dve, "s_esink", before("self", i))
                    nc.vector.tensor_reduce(max_s[:], SC[0].rearrange("p b (h k) -> p (b h) k", k=P), AX.X, ALU.max).then_inc(S["s_rowmax"], 1)
                    wait(dve, "s_rowmax", ns)
                    nc.vector.tensor_scalar(max_s[:], max_s[:], sink, None, ALU.max).then_inc(S["s_max"], 1)
                    wait(dve, "s_max", ns)
                    wait(dve, "s_tr", before("self", i), 2)
                    nc.vector.tensor_tensor(z_s[:], SC[0].rearrange("p b (h k) -> p (b h) k", k=P),
                                            max_s[:].rearrange("p (h a) -> p h a", a=1).to_broadcast([P, H, P]), ALU.subtract).then_inc(S["s_z"], 1)
                if runs("cross", i):
                    wait(dve, "x_kv_ps", nx)
                    wait(dve, "x_sc", before("cross", i), 2)
                    nc.vector.scalar_tensor_tensor(out=k_x[:], in0=M1[:, 0:SK].rearrange("p (a k) -> p a k", a=1).to_broadcast([P, 4, SK]), scalar=bx_k,
                                                   in1=half_x.rearrange("p (h a) -> p h a", a=1).to_broadcast([P, 4, SK]),
                                                   op0=ALU.add, op1=ALU.mult).then_inc(S["x_k"], 1)
                    wait(dve, "x_pv", before("cross", i))
                    nc.vector.tensor_tensor(v_x[0:SK, :, 0:XD], M1[0:SK, P:2 * P].rearrange("p (h d) -> p h d", h=XH),
                                            bx_v[0:SK, :].rearrange("p (h d) -> p h d", h=XH), ALU.add).then_inc(S["x_v"], 1)
                if runs("ffn", i):
                    wait(dve, "f_rank_ps", nf)
                    wait(dve, "f_pick", before("ffn", i))
                    nc.vector.tensor_tensor(place[:], M1[:, 0:E], base[:], ALU.add).then_inc(S["f_place"], 1)
                    wait(dve, "f_place", nf)
                    nc.vector.tensor_tensor(base[:], M1[:, E:2 * E], base[:], ALU.add).then_inc(S["f_base"], 1)
                    nc.vector.tensor_tensor(picked[:], hot[:], place[:].rearrange("p (a e) -> p a e", a=1).to_broadcast([P, 2, E]),
                                            ALU.mult).then_inc(S["f_pick"], 1)
                    wait(dve, "f_pick", nf)
                    nc.vector.tensor_reduce(row_f[:], picked[:], AX.X, ALU.add).then_inc(S["f_rowf"], 1)
                    wait(dve, "f_rowf", nf)
                    wait(dve, "f_sent", before("ffn", i), 32)
                    nc.vector.tensor_copy(row_i[:], row_f[:]).then_inc(S["f_row"], 1)
                    nc.vector.tensor_copy(tile(ROW, "ffn", i), row_f[:]).then_inc(S["f_rowlog"], 1)

                def cross_max(half):
                    scores = SC[1 - half][:, :, 0:4 * SK].rearrange("p b (h k) -> p b h k", k=SK)
                    part = slice(8 * half, 8 * half + 8)
                    wait_part(dve, "x_sc", nx, 2, half)
                    nc.vector.tensor_reduce(max_x[:, part], scores, AX.X, ALU.max).then_inc(S["x_max"], 1)
                    wait_part(dve, "x_max", nx, 2, half)
                    wait(dve, "x_tr", before("cross", i), 4)
                    nc.vector.tensor_tensor(z_x[:, part, :].rearrange("p (b h) k -> p b h k", b=2), scores,
                                            max_x[:, part].rearrange("p (b h a) -> p b h a", b=2, a=1).to_broadcast([P, 2, 4, SK]),
                                            ALU.subtract).then_inc(S["x_z"], 1)

                if runs("cross", i):
                    cross_max(0)
                if runs("ffn", i):
                    wait(dve, "f_th", nf)
                    nc.vector.scalar_tensor_tensor(out=g_f[:], in0=th_f[:], scalar=1.0, in1=M0[:, 0:SH], op0=ALU.add, op1=ALU.mult).then_inc(S["f_g"], 1)
                    wait(dve, "f_g", nf)
                    wait(dve, "f_hT_ps", before("ffn", i))
                    nc.vector.tensor_tensor(h_f[:], M0[:, SH:2 * SH], g_f[:], ALU.mult).then_inc(S["f_h"], 1)
                if runs("self", i):
                    wait(dve, "s_pv", ns)
                    wait(dve, "s_esink", ns)
                    o = M1[:, 0:H * (HD + 1)].rearrange("p (h d) -> p h d", h=H)
                    nc.vector.tensor_tensor(den_s[:], o[:, :, HD:HD + 1].rearrange("p h a -> p (h a)"), esink[:], ALU.add).then_inc(S["s_den"], 1)
                    wait(dve, "s_den", ns)
                    nc.vector.reciprocal(den_s[:], den_s[:]).then_inc(S["s_rden"], 1)
                    wait(dve, "s_rden", ns)
                    wait(dve, "s_oT_ps", before("self", i))
                    nc.vector.tensor_tensor(o_s[:], o[:, :, 0:HD], den_s[:].rearrange("p (h a) -> p h a", a=1).to_broadcast([P, H, HD]),
                                            ALU.mult).then_inc(S["s_o"], 1)
                if runs("ln3", i):
                    met(dve)
                    wait(dve, "x_done", done("ln3", i))
                    layer_norm("ln3", i)
                if runs("ln1", i):
                    met(dve)
                    wait(dve, "x_in", done("ln1", i), 16)
                    layer_norm("ln1", i)
                if runs("cross", i):
                    cross_max(1)
                if runs("ln3", i):
                    normed("ln3", i, [("f_xT_ps", done("ffn", i), 1), ("f_sent", done("ffn", i), 32)])
                if runs("ln1", i):
                    normed("ln1", i, [("s_xT_ps", done("self", i), 1)])
                if runs("ffn", i):
                    wait(dve, "f_dn_ps", nf)
                    nc.vector.tensor_tensor(tile(X, "ffn", i), M0[:, 0:D], tile(X, "ffn", i), ALU.add).then_inc(S["f_done"], 1)
                if runs("self", i):
                    wait(dve, "s_out_ps", ns)
                    wait(dve, "s_xb", ns)
                    nc.vector.tensor_tensor(tile(X, "self", i), M1[:, 0:D], xb_s[:], ALU.add).then_inc(S["s_done"], 1)
                if runs("ln2", i):
                    met(dve)
                    wait(dve, "s_done", ns)
                    layer_norm("ln2", i)
                    normed("ln2", i, [("x_T_ps", done("cross", i), 1)])
                if runs("cross", i):
                    wait(dve, "x_pv", nx)
                    o = M0[:, 0:XH * (XD + 1)].rearrange("p (h d) -> p h d", h=XH)
                    nc.vector.reciprocal(den_x[:], o[:, :, XD:XD + 1].rearrange("p h a -> p (h a)")).then_inc(S["x_rden"], 1)
                    wait(dve, "x_rden", nx)
                    wait(dve, "x_oT_ps", done("xout", i))
                    nc.vector.tensor_tensor(o_x[:], o[:, :, 0:XD], den_x[:].rearrange("p (h a) -> p h a", a=1).to_broadcast([P, XH, XD]),
                                            ALU.mult).then_inc(S["x_o"], 1)

            steps_of(dve, step)

            chain = [0]

            def link(ins):
                chain[0] += 1
                ins.then_inc(S["t_step"], 1)
                dve.wait_ge(S["t_step"], chain[0])

            dve.wait_ge(S["w_late"], 16 * 3)
            dve.wait_ge(S["f_base"], TILES)
            nc.vector.tensor_copy(tail[:], base[0:1, :]).then_inc(S["t_tail"], 1)
            link(nc.vector.tensor_tensor(count[:], base[:], base0, ALU.subtract))
            link(nc.vector.tensor_tensor(full[:], count[:].rearrange("p (e a) -> p e a", a=1).to_broadcast([P, E, TILES]),
                                         steps.rearrange("p (a n) -> p a n", a=1).to_broadcast([P, E, TILES]), ALU.is_gt))
            link(nc.vector.tensor_reduce(n_blk[:], full[:], AX.X, ALU.add))
            link(nc.vector.tensor_copy(ends[:, 0:1], n_blk[:, 0:1]))
            for e in range(1, E):
                link(nc.vector.tensor_tensor(ends[:, e:e + 1], ends[:, e - 1:e], n_blk[:, e:e + 1], ALU.add))
            blk = blocks[:].rearrange("p (t a) -> p t a", a=1).to_broadcast([1, BLOCKS, E])
            link(nc.vector.tensor_tensor(past[:], blk, ends[0:1, :].rearrange("p (a e) -> p a e", a=1).to_broadcast([1, BLOCKS, E]), ALU.is_ge))
            link(nc.vector.tensor_reduce(of[:], past[:], AX.X, ALU.add))
            link(nc.vector.tensor_tensor(past[:], past[:], n_blk[0:1, :].rearrange("p (a e) -> p a e", a=1).to_broadcast([1, BLOCKS, E]), ALU.mult))
            link(nc.vector.tensor_reduce(at[:], past[:], AX.X, ALU.add))
            link(nc.vector.tensor_tensor(at[:], blocks[:], at[:], ALU.subtract))
            link(nc.vector.tensor_scalar(at[:], at[:], float(P), None, ALU.mult))
            link(nc.vector.tensor_scalar(off_f[:, 0, :], of[:], float(REGION), None, ALU.mult))
            link(nc.vector.tensor_tensor(off_f[:, 0, :], off_f[:, 0, :], at[:], ALU.add))
            link(nc.vector.tensor_scalar(of[:], of[:], float(E - 1), None, ALU.min))
            link(nc.vector.tensor_scalar(off_f[:, 1, :], of[:], float(2 * EH), None, ALU.mult))
            link(nc.vector.tensor_scalar(off_f[:, 2, :], of[:], float(D), None, ALU.mult))
            nc.vector.tensor_copy(table[:], off_f[:]).then_inc(S["t_table"], 1)
            link(nc.vector.tensor_scalar(jump[:], n_blk[:], float(P), -float(REGION), ALU.mult, ALU.add))
            row_of = ROW[:].rearrange("p t s -> p (t s)")
            link(nc.vector.tensor_tensor(passed_e[:], row_of.rearrange("p (n a) -> p n a", a=1).to_broadcast([P, 2 * TILES, E - 1]),
                                         base0[:, 1:E].rearrange("p (a e) -> p a e", a=1).to_broadcast([P, 2 * TILES, E - 1]), ALU.is_ge))
            link(nc.vector.tensor_tensor(passed_e[:], passed_e[:],
                                         jump[:, 0:E - 1].rearrange("p (a e) -> p a e", a=1).to_broadcast([P, 2 * TILES, E - 1]), ALU.mult))
            link(nc.vector.tensor_reduce(shift[:], passed_e[:], AX.X, ALU.add))
            nc.vector.tensor_tensor(MADE[:].rearrange("p t s -> p (t s)"), row_of, shift[:], ALU.add).then_inc(S["t_made"], 1)

            XT, GU, HT, Y = (PS[:, b, :] for b in range(4))
            gu = GU.rearrange("p (a n) -> p a n", a=2)

            def pair(j, u):
                static = isinstance(j, int)
                if not static or 0 <= j - 3 < PAIRS:
                    dve.wait_ge(S["e_y_ps"], j - 2)
                    w = (u - 3) % RING
                    if not static:
                        dve.wait_ge(S[f"e_out{w}"], (j - u) * (16 // RING) - (16 if u < 3 else 0))
                    elif j - 3 >= RING:
                        dve.wait_ge(S[f"e_out{w}"], (j - 3) // RING * 16)
                    nc.vector.tensor_copy(rows_out[:, w, :, :].rearrange("p a d -> p (a d)"), Y[:, 0:2 * D]).then_inc(S["e_y"], 1)
                if not static or 0 <= j - 1 < PAIRS:
                    dve.wait_ge(S["e_th"], j)
                    nc.vector.scalar_tensor_tensor(out=g_e[:], in0=th_e[:], scalar=1.0, in1=gu[:, :, 0:EH], op0=ALU.add, op1=ALU.mult).then_inc(S["e_g"], 1)
                    dve.wait_ge(S["e_g"], j)
                    if not static or j - 1 > 0:
                        dve.wait_ge(S["e_hT_ps"], j - 1)
                    nc.vector.tensor_tensor(h_e[:], gu[:, :, EH:2 * EH], g_e[:], ALU.mult).then_inc(S["e_h"], 1)

            pairs_of(dve, pair)

            dve.wait_ge(S["f_gate"], TILES)
            nc.vector.tensor_scalar(GATE[:], GATE[:], 0.5, 0.5, ALU.mult, ALU.add).then_inc(S["g_gate"], 1)
            dve.wait_ge(S["g_gate"], 1)
            with dve.Fori(0, TILES // GRING) as r:
                for u in range(GRING):
                    t = r * GRING
                    x_t = X[:, bass.ds(t + u, 1), :].rearrange("p a d -> p (a d)")
                    gate = GATE[:, bass.ds(t + u, 1), :].rearrange("p a s -> p (a s)")
                    dve.wait_ge(S[f"g_back{u}"], r * 32 + 32)
                    nc.vector.scalar_tensor_tensor(out=summed[:, u, :], in0=back[:, u, 0, :], scalar=gate[:, 0:1], in1=x_t,
                                                   op0=ALU.mult, op1=ALU.add).then_inc(S["g_sum"], 1)
                    dve.wait_ge(S["g_sum"], t + (u + 1))
                    nc.vector.scalar_tensor_tensor(out=x_t, in0=back[:, u, 1, :], scalar=gate[:, 1:2], in1=summed[:, u, :],
                                                   op0=ALU.mult, op1=ALU.add).then_inc(S["g_done"], 1)

        @block.gpsimd
        def _(pool):
            pool.wait_ge(S["s_const"], 5)
            pool.wait_ge(S["w_early"], 16 * (EARLY + 3))
            nc.gpsimd.tensor_scalar(w_sdown[:], w_sdown[:], 0.5, 1.0, ALU.mult, ALU.mult).then_inc(S["w_half"], 1)

            def root(ln, i):
                n, last = done(ln, i), before(ln, i)
                wait(pool, ln + "_mv", n)
                wait(pool, ln + "_rstd", last)
                passed(pool)
                nc.gpsimd.tensor_scalar(var[ln][:], mv[ln][:, 1:2], EPS, 1.0, ALU.add, ALU.mult).then_inc(S[ln + "_var"], 1)
                wait(pool, ln + "_x", last)
                wait(pool, ln + "_var", n)
                nc.gpsimd.tensor_tensor(rstd[ln][:], var[ln][:], minus_half[:], ALU.pow).then_inc(S[ln + "_rstd"], 1)

            def step(i):
                if runs("xout", i):
                    wait(pool, "x_done", before("xout", i))
                    nc.gpsimd.tensor_tensor(xb_x[:], tile(X, "xout", i), bx_o[:], ALU.add).then_inc(S["x_xb"], 1)
                if runs("self", i):
                    wait(pool, "x_in", done("self", i), 16)
                    wait(pool, "s_done", before("self", i))
                    nc.gpsimd.tensor_tensor(xb_s[:], tile(X, "self", i), b_o[:], ALU.add).then_inc(S["s_xb"], 1)
                if runs("ffn", i):
                    met(pool)
                    wait(pool, "f_row", done("ffn", i))
                    wait(pool, "ln3_x", done("ffn", i))
                    for s in range(2):
                        nc.gpsimd.indirect_dma_start(sent[:, :], bass.IndirectOffsetOnAxis(row_i[:, s:s + 1], 0), xn["ln3"][:], None).then_inc(S["f_sent"], 16)
                if runs("ln3", i):
                    root("ln3", i)
                if runs("ln1", i):
                    root("ln1", i)
                if runs("ln2", i):
                    root("ln2", i)

            steps_of(pool, step)
            pool.wait_ge(S["w_late"], 16 * 3)
            nc.gpsimd.tensor_scalar(w_down[:], w_down[:], 0.5, 1.0, ALU.mult, ALU.mult).then_inc(S["w_half"], 1)
            pool.wait_ge(S["f_rowlog"], TILES)
            blocks_of = made.rearrange("(j a p) d -> j p a d", a=2, p=P)
            with pool.Fori(0, PAIRS // RING) as r:
                for u in range(RING):
                    pool.wait_ge(S["e_y"], r * RING + (u + 1))
                    passed(pool)
                    pool.dma_start(blocks_of[bass.ds(r * RING + u, 1), :, :, :].rearrange("j p a d -> p (j a) d"),
                                   rows_out[:, u, :, :]).then_inc(S[f"e_out{u}"], 16)
            for u in range(RING):
                pool.wait_ge(S[f"e_out{u}"], 16 * (PAIRS // RING))
            pool.wait_ge(S["t_made"], 1)

            def gather(t, u):
                src = MADE[:, t, :] if isinstance(t, int) else MADE[:, bass.ds(t, 1), :].rearrange("p a s -> p (a s)")
                nc.gpsimd.tensor_copy(idx[:, u, :], src).then_inc(S["g_idx"], 1)
                pool.wait_ge(S["g_idx"], t + 1)
                passed(pool)
                for s in range(2):
                    nc.gpsimd.indirect_dma_start(back[:, u, s, :], None, made[:, :], bass.IndirectOffsetOnAxis(idx[:, u, s:s + 1], 0)).then_inc(S[f"g_back{u}"], 16)

            for t in range(GRING):
                gather(t, t)
            with pool.Fori(1, TILES // GRING) as r:
                for u in range(GRING):
                    met(pool)
                    pool.wait_ge(S["g_done"], r * GRING + (u + 1 - GRING))
                    gather(r * GRING + u, u)


def kernel(**inputs):
    import concourse.bacc as bacc
    from concourse.bass_utils import run_bass_kernel_spmd

    a = {n: np.asarray(v) for n, v in inputs.items()}
    arrays = {
        "x": a["x"], "ctx": a["ctx_1024"], "sink": a["L0_attn_sink_bias"].reshape(1),
        "wq": a["L0_attn_Wq"].T, "wk": a["L0_attn_Wk"].T, "wv": a["L0_attn_Wv"].T, "wo": a["L0_attn_Wo"].T,
        "bq": a["L0_attn_bq"], "bk": a["L0_attn_bk"], "bv": a["L0_attn_bv"], "bo": a["L0_attn_bo"],
        "xwq": a["L0_xattn_wq"].T, "xwk": a["L0_xattn_wk"].T, "xwv": a["L0_xattn_wv"].T, "xwo": a["L0_xattn_wo"].T,
        "xbq": a["L0_xattn_bq"], "xbk": a["L0_xattn_bk"], "xbv": a["L0_xattn_bv"], "xbo": a["L0_xattn_bo"],
        "router": a["L0_ffn_router_w"].T, "gate_up": a["L0_ffn_gate_up_w"], "down": a["L0_ffn_down_w"],
        "shared_gate": a["L0_ffn_shared_gate_w"].T, "shared_up": a["L0_ffn_shared_up_w"].T, "shared_down": a["L0_ffn_shared_down_w"].T,
    }
    arrays.update(constants())
    arrays = {n: np.ascontiguousarray(v) for n, v in arrays.items()}
    nc = bacc.Bacc("TRN2", target_bir_lowering=False, num_devices=1)
    aps = {n: nc.dram_tensor(n, v.shape, mybir.dt.from_np(v.dtype), kind="ExternalInput").ap() for n, v in arrays.items()}
    out = nc.dram_tensor("out", [TILES, P, D], F32, kind="ExternalOutput").ap()
    decoder_program(nc, aps, out)
    r = run_bass_kernel_spmd(nc, [arrays], core_ids=[0])
    return r.results[0]["out"]
```

```python
from contextlib import ExitStack

import numpy as np

import concourse.bass as bass
from concourse import mybir

F32 = mybir.dt.float32
F16 = mybir.dt.float16
BF16 = mybir.dt.bfloat16
U32 = mybir.dt.uint32
I32 = mybir.dt.int32
ALU = mybir.AluOpType
ACT = mybir.ActivationFunctionType
AX = mybir.AxisListType

TILES, P, D = 64, 128, 128
SK = 120
H, KV, HD = 8, 2, 16
WIN = 32
XH, XD = 16, 8
E, EH = 16, 128
SH = 256
EPS = 1e-5
FP16_MIN = -65504.0
REGION = TILES * P + P
DUMMY = E * REGION
BLOCKS = (2 * TILES * P + E * (P - 1)) // P + 1
PAIRS = BLOCKS // 2
SPARE = BLOCKS - 2 * TILES
ROWS = DUMMY + SPARE * P
W = D + 1
TOKENS = TILES * P
RING = 8
GRING = 4

SKEW = {"ln1": -2, "sproj": -1, "self": 0, "ln2": 0, "xproj": 1, "cross": 2, "xout": 3, "ln3": 3, "ffn": 4}
FIRST_STEP, LAST_STEP = -2, TILES + 3
AHEAD = 4
CONSTANTS = 13
EARLY = 37
LOOP_FROM, LOOP_TO = 5, TILES - 2


def constants():
    p = np.arange(P)
    band = (p[None, :] <= p[:, None]) & (p[None, :] > p[:, None] - WIN)
    small = np.zeros((P, 128), np.float32)
    small[:, 64:128] = np.arange(TILES) * P
    small[:, 38:42] = (p[:, None] % 64 // HD) == np.arange(4)
    small[:, 2:6] = (p[:, None] % 32 // XD) == np.arange(4)
    small[:, 6:22] = np.arange(E)
    small[:, 22:38] = np.arange(E) * REGION
    return {
        "c_ident": np.eye(P, dtype=np.float32),
        "c_band": np.concatenate([np.eye(P), np.where(band, 0.0, FP16_MIN)], 1).astype(np.float16),
        "c_tri": np.concatenate([p[:, None] < p[None, :], np.ones((P, P))], 1).astype(np.float16),
        "c_small": small,
        "c_dest": (2 * (np.arange(TILES)[None, :, None] * P + p[:, None, None]) + np.arange(2)).astype(np.uint32),
        "c_fill": np.concatenate([np.zeros(((E + SPARE) * P, D)), 2 * TOKENS + np.arange((E + SPARE) * P)[:, None]], 1).astype(np.uint32),
        "c_blocks": np.arange(BLOCKS, dtype=np.float32)[None, :],
    }


def decoder_program(nc, A, out):
    sent = nc.dram_tensor("sent_rows", [ROWS, W], F32, kind="Internal").ap()
    made = nc.dram_tensor("made_rows", [2 * TOKENS + (E + SPARE) * P, D], F32, kind="Internal").ap()

    with ExitStack() as ctx:
        def sb(name, shape, dt=F32):
            return ctx.enter_context(nc.sbuf_tensor(name, shape, dt))

        def sem(name):
            return ctx.enter_context(nc.semaphore(name))

        X = sb("X", [P, TILES, D])
        ctx_now = sb("ctx_now", [SK, D])
        w_sq = sb("w_sq", [P, P]); w_sk = sb("w_sk", [P, P]); w_sv = sb("w_sv", [P, KV * HD]); w_so = sb("w_so", [P, P])
        w_xq = sb("w_xq", [P, P]); w_xk = sb("w_xk", [P, P]); w_xv = sb("w_xv", [P, P]); w_xo = sb("w_xo", [P, P])
        w_router = sb("w_router", [P, E])
        w_shared = sb("w_shared", [P, 2 * SH])
        w_sdown = sb("w_sdown", [P, 2, D])
        w_up = sb("w_up", [P, E, 2 * EH])
        w_down = sb("w_down", [P, E, D])
        b_cols = sb("b_cols", [P, 6])
        b_q, b_k, bx_q, bx_k, sink, b_q4 = (b_cols[:, n:n + 1] for n in range(6))
        b_v = sb("b_v", [P, KV * HD]); b_o = sb("b_o", [P, D]); bx_v = sb("bx_v", [P, D]); bx_o = sb("bx_o", [P, D])
        ident = sb("ident", [P, P]); band = sb("band", [P, 2, P], F16); tri = sb("tri", [P, 2, P], F16)
        small = sb("small", [P, 128])
        half_s, half_x, iota_e, base0, steps = small[:, 38:42], small[:, 2:6], small[:, 6:22], small[:, 22:38], small[:, 64:128]
        minus_half = sb("minus_half", [P, 1])
        dest = sb("dest", [P, TILES, 2], U32)
        bk_half = sb("bk_half", [P, 4]); bxk_half = sb("bxk_half", [P, 4]); minus_sink = sb("minus_sink", [P, 1])
        ones_s = sb("ones_s", [P, 2, 32]); ones_x = sb("ones_x", [P, 4, 32])
        stats = {n: sb(f"stats_{n}", [P, 6]) for n in ("ln1", "ln2", "ln3")}
        mv = {n: sb(f"mv_{n}", [P, 2]) for n in ("ln1", "ln2", "ln3")}
        var = {n: sb(f"var_{n}", [P, 1]) for n in ("ln1", "ln2", "ln3")}
        rstd = {n: sb(f"rstd_{n}", [P, 1]) for n in ("ln1", "ln2", "ln3")}
        xn = {n: sb(f"xn_{n}", [P, D]) for n in ("ln1", "ln2", "ln3")}
        shift = {n: sb(f"shift_{n}", [P, 1]) for n in ("ln1", "ln2", "ln3")}
        rows_sent = sb("rows_sent", [P, 2, W])
        xT_s = sb("xT_s", [P, P]); q_s = sb("q_s", [P, P]); k_s = sb("k_s", [P, 4, P])
        v_s = sb("v_s", [P, KV, 2, 32])
        rowmax = sb("rowmax", [P, H]); nmax_s = sb("nmax_s", [P, H]); esink = sb("esink", [P, H, HD]); z_s = sb("z_s", [P, H, P]); e_s = sb("e_s", [P, H, P])
        rden_s = sb("rden_s", [P, P]); oT_s = sb("oT_s", [P, P]); xb_s = sb("xb_s", [P, D])
        xcT = sb("xcT", [P, P + SK]); q_x = sb("q_x", [P, P]); k_x = sb("k_x", [P, 4, SK])
        v_x = sb("v_x", [P, 4, 4, 32])
        max_x = sb("max_x", [P, XH]); z_x = sb("z_x", [P, XH, SK]); e_x = sb("e_x", [P, XH, P])
        rden_x = sb("rden_x", [P, P]); oT_x = sb("oT_x", [P, P]); xb_x = sb("xb_x", [P, D])
        xT_f = sb("xT_f", [P, P]); th_f = sb("th_f", [P, SH]); g_f = sb("g_f", [P, SH]); h_f = sb("h_f", [P, SH]); hT_f = sb("hT_f", [P, 2, P])
        logit = sb("logit", [P, E]); top = sb("top", [P, 8]); top_i = sb("top_i", [P, 8], U32); top_f = sb("top_f", [P, 2])
        hot = sb("hot", [P, 2, E]); hots = sb("hots", [P, E], F16); base = sb("base", [P, E]); place = sb("place", [P, E])
        picked = sb("picked", [P, 2, E]); row_f = sb("row_f", [P, 2]); row_i = sb("row_i", [P, 2], U32)
        GATE = sb("GATE", [P, TILES, 2])
        blocks = sb("blocks", [1, BLOCKS]); 
        count = sb("count", [P, E]); full = sb("full", [P, E, TILES]); n_blk = sb("n_blk", [P, E]); ends = sb("ends", [P, E])
        past = sb("past", [1, BLOCKS, E]); of = sb("of", [1, BLOCKS]); at = sb("at", [1, BLOCKS]); live = sb("live", [1, BLOCKS])
        off_f = sb("off_f", [1, 3, BLOCKS]); table = sb("table", [1, 3, BLOCKS], I32)
        tail = sb("tail", [1, E], I32)
        rows_in = sb("rows_in", [P, RING, 2, W]); xT_e = sb("xT_e", [P, 2, P]); th_e = sb("th_e", [P, 2, EH])
        g_e = sb("g_e", [P, 2, EH]); h_e = sb("h_e", [P, 2, EH]); hT_e = sb("hT_e", [P, 2, P]); rows_out = sb("rows_out", [P, RING, 2, D])
        back = sb("back", [P, GRING, 2, D]); summed = sb("summed", [P, GRING, D])

        PS = ctx.enter_context(nc.psum_tensor("PS", [P, 8, 512], F32))
        SC = [PS[:, 0:2, :], PS[:, 2:4, :]]
        TR = [PS[:, 4, :], PS[:, 5, :]]
        M0, M1, M2, M3 = (PS[:, b, :] for b in (6, 7, 2, 3))

        names = """w_early w_late s_const b_ready x_in ctx_in zeroed passed
            ln1_stats ln1_mv ln1_var ln1_shift ln1_rstd ln1_x ln2_stats ln2_mv ln2_var ln2_rstd ln2_shift ln2_x
            ln3_stats ln3_mv ln3_var ln3_shift ln3_rstd ln3_x ln3_dest ln3_sent
            s_xT_ps s_xT s_qk_ps s_q s_k s_v_ps s_v s_sc s_rowmax s_max s_z s_esink s_tr s_e s_pv s_rden s_oT s_out_ps s_xb s_done
            x_T_ps x_T x_qk_ps x_q x_k x_v_ps x_v x_sc x_max x_z x_tr x_e x_pv x_rden x_oT x_out_ps x_xb x_done
            f_xT_ps f_xT f_lg_ps f_logit f_top f_topi f_topf f_hot f_hots f_gate f_gu_ps f_th f_g f_h f_rank_ps f_place f_base f_pick f_rowf f_row f_sent
            f_hT_ps f_hT f_dn_ps f_done
            t_step t_table t_tail w_half e_xT_ps e_xT e_gu_ps e_th e_g e_h e_hT_ps e_hT e_y_ps e_y
            g_gate g_sum g_done g_out""".split()
        S = {n: sem(n) for n in names}
        for u in range(RING):
            S[f"e_in{u}"] = sem(f"e_in{u}")
            S[f"e_out{u}"] = sem(f"e_out{u}")
        for u in range(GRING):
            S[f"g_back{u}"] = sem(f"g_back{u}")

        def at_block(row, j, a):
            return table[0:1, row, 2 * j + a:2 * j + a + 1] if isinstance(j, int) else table[0:1, row, bass.ds(j * 2 + a, 1)]

        def steps_of(eng, body):
            for i in range(FIRST_STEP, LOOP_FROM):
                body(i)
            with eng.Fori(LOOP_FROM, LOOP_TO) as i:
                body(i)
            for i in range(LOOP_TO, LAST_STEP + 1):
                body(i)

        def runs(stage, i):
            return not isinstance(i, int) or 0 <= i - SKEW[stage] < TILES

        def done(stage, i):
            n = i - SKEW[stage] + 1
            return max(0, min(TILES, n)) if isinstance(i, int) else n

        def before(stage, i):
            return done(stage, i - 1)

        def wait(eng, name, n, per=1):
            if isinstance(n, int) and n <= 0:
                return
            eng.wait_ge(S[name], n * per if per != 1 else n)

        def tile(buf, stage, i):
            t = i - SKEW[stage]
            return buf[:, t, :] if isinstance(t, int) else buf[:, bass.ds(t, 1), :].rearrange("p a d -> p (a d)")

        def passed(eng):
            eng.sem_inc(S["passed"], 1)

        def met(eng):
            eng.wait_ge(S["s_const"], CONSTANTS)

        def wait_part(eng, name, n, parts, c):
            eng.wait_ge(S[name], n * parts - (parts - 1 - c))

        def pairs_of(eng, body):
            for j in range(2 * RING):
                body(j, j % RING)
            with eng.Fori(2, PAIRS // RING) as r:
                for u in range(RING):
                    body(r * RING + u, u)
            for j in range(PAIRS, PAIRS + 3):
                body(j, j % RING)

        def own_block(v):
            a = v[0:SK]
            return bass.AP(tensor=a.tensor, offset=a.offset, ap=[[4 * 4 * 32, SK], [4 * 32, 4], [32 + XD, 4], [1, XD]])

        block = ctx.enter_context(nc.Block())

        @block.sync
        def _(sp):
            n = 0
            for dst, src in ((ident, A["c_ident"]), (w_sq, A["wq"]), (small, A["c_small"]),
                             (w_sv, A["wv"]), (band, A["c_band"].rearrange("p (a b) -> p a b", a=2)), (w_so, A["wo"]),
                             (w_xq, A["xwq"]), (w_xk, A["xwk"]), (w_xv, A["xwv"]), (w_xo, A["xwo"]),
                             (w_router, A["router"]), (dest, A["c_dest"]), (tri, A["c_tri"].rearrange("p (a b) -> p a b", a=2))):
                sp.dma_start(dst[:], src).then_inc(S["w_early"], 16)
                n += 1
            for h in range(H):
                kv = h // (H // KV)
                sp.dma_start(w_sk[:, h * HD:(h + 1) * HD], A["wk"][:, kv * HD:(kv + 1) * HD]).then_inc(S["w_early"], 16)
                sp.dma_start(b_k[h * HD:(h + 1) * HD, :], A["bk"][kv * HD:(kv + 1) * HD].rearrange("(p a) -> p a", a=1)).then_inc(S["w_early"], 16)
                n += 2
            for dst, src in ((b_q, A["bq"]), (bx_q, A["xbq"]), (bx_k, A["xbk"])):
                sp.dma_start(dst, src.rearrange("(p a) -> p a", a=1)).then_inc(S["w_early"], 16)
                n += 1
            for dst, src in ((b_v, A["bv"]), (b_o, A["bo"]), (bx_v, A["xbv"]), (bx_o, A["xbo"]), (sink, A["sink"])):
                sp.dma_start(dst[:], src.rearrange("(a n) -> a n", a=1).to_broadcast([P, src.shape[0]])).then_inc(S["w_early"], 16)
                n += 1
            assert n == EARLY
            for dst, src in ((w_shared[:, 0:SH], A["shared_gate"]), (w_shared[:, SH:], A["shared_up"]),
                             (w_sdown, A["shared_down"].rearrange("(c p) d -> p c d", p=P))):
                sp.dma_start(dst[:], src).then_inc(S["w_early"], 16)
            for t in range(AHEAD):
                sp.dma_start(X[:, t, :], A["x"][t, :, :]).then_inc(S["x_in"], 16)
                sp.wait_ge(S["x_in"], t * 16 + 16)
            for dst, src in ((w_up, A["gate_up"].rearrange("e p n -> p e n")), (w_down, A["down"].rearrange("e p n -> p e n")),
                             (blocks, A["c_blocks"])):
                sp.dma_start(dst[:], src).then_inc(S["w_late"], 16)
            sp.dma_start(ctx_now[:], A["ctx"][0, :, :]).then_inc(S["ctx_in"], 16)
            with sp.Fori(1, TILES - AHEAD + 1) as t:
                sp.dma_start(X[:, bass.ds(t + (AHEAD - 1), 1), :], A["x"][bass.ds(t + (AHEAD - 1), 1), :, :].rearrange("a p d -> p a d")).then_inc(S["x_in"], 16)
                sp.wait_ge(S["x_T_ps"], t)
                sp.dma_start(ctx_now[:], A["ctx"][bass.ds(t, 1), :, :].rearrange("a p d -> p (a d)")).then_inc(S["ctx_in"], 16)
                sp.wait_ge(S["x_in"], t * 16 + AHEAD * 16)
                passed(sp)
            for t in range(TILES - AHEAD + 1, TILES):
                sp.wait_ge(S["x_T_ps"], t)
                sp.dma_start(ctx_now[:], A["ctx"][t, :, :]).then_inc(S["ctx_in"], 16)
            for b in range(SPARE):
                sp.dma_start(sent[DUMMY + b * P:DUMMY + (b + 1) * P, :], A["c_fill"][(E + b) * P:(E + b + 1) * P, :].bitcast(F32)).then_inc(S["zeroed"], 16)
            sp.wait_ge(S["t_tail"], 1)
            for e in range(E):
                r = sp.value_load(tail[0:1, e:e + 1], min_val=0, max_val=DUMMY - P)
                sp.dma_start(sent[bass.ds(r, P), :], A["c_fill"][e * P:(e + 1) * P, :].bitcast(F32)).then_inc(S["zeroed"], 16)
            sp.wait_ge(S["zeroed"], 16 * (SPARE + E))
            sp.wait_ge(S["f_sent"], 32 * TILES)
            sp.wait_ge(S["t_table"], 1)

            def load(j, u):
                for a in range(2):
                    r = sp.value_load(at_block(0, j, a), min_val=0, max_val=ROWS - P)
                    sp.dma_start(rows_in[:, u, a, :], sent[bass.ds(r, P), :]).then_inc(S[f"e_in{u}"], 16)

            for j in range(RING):
                load(j, j)
            with sp.Fori(1, PAIRS // RING) as r:
                for u in range(RING):
                    sp.wait_ge(S[f"e_out{u}"], r * 32)
                    load(r * RING + u, u)
            for u in range(RING):
                sp.wait_ge(S[f"e_out{u}"], 32 * (PAIRS // RING))

            def fetch(t, u):
                src = made[t * 2 * P:(t + 1) * 2 * P, :] if isinstance(t, int) else made[bass.ds(t * (2 * P), 2 * P), :]
                sp.dma_start(back[:, u, :, :], src.rearrange("(p s) d -> p s d", s=2)).then_inc(S[f"g_back{u}"], 16)

            for t in range(GRING):
                fetch(t, t)
            with sp.Fori(1, TILES // GRING) as r:
                for u in range(GRING):
                    sp.wait_ge(S["g_done"], r * GRING + (u + 1 - GRING))
                    fetch(r * GRING + u, u)

        @block.tensor
        def _(pe):
            pe.wait_ge(S["w_early"], 16 * (EARLY + 3))

            pe.wait_ge(S["w_half"], 1)

            def step(i):
                n_sp, n_s, n_xp, n_x, n_xo, n_f = (done(s, i) for s in ("sproj", "self", "xproj", "cross", "xout", "ffn"))
                b_sp, b_s, b_xp, b_x, b_xo, b_f = (before(s, i) for s in ("sproj", "self", "xproj", "cross", "xout", "ffn"))

                def read(*readers):
                    for name, n, per in readers[:1] if not isinstance(i, int) else readers:
                        wait(pe, name, n, per)

                def cross_scores(half):
                    for b in range(2):
                        g = 2 * half + b
                        mm = pe.matmul(SC[1 - half][:, b, 0:4 * SK], q_x[32 * g:32 * g + 32, :],
                                       k_x[32 * g:32 * g + 32, :, :].rearrange("p h k -> p (h k)"),
                                       start=True, stop=True, tile_position=(32 * g, 0))
                    mm.then_inc(S["x_sc"], 1)

                def cross_transposes(c):
                    wait_part(pe, "x_z", n_x, 2, c // 2)
                    if c < 2:
                        wait_part(pe, "s_e", n_s, 2, c) if runs("self", i) else wait(pe, "s_e", n_s, 2)
                        if isinstance(i, int):
                            wait(pe, "x_e", b_x, 4)
                    else:
                        wait_part(pe, "x_e", n_x, 4, c - 2)
                    for j in range(4):
                        mm = pe.transpose(TR[c % 2][0:SK, j * P:(j + 1) * P], z_x[:, 4 * c + j, :], ident[:])
                    mm.then_inc(S["x_tr"], 1)

                if runs("self", i):
                    wait(pe, "s_q", n_s)
                    wait(pe, "s_k", n_s)
                    read(("x_z", b_x, 2), ("s_z", b_s, 1))
                    for b in range(2):
                        pe.matmul(SC[0][:, b, :].rearrange("p (h k) -> p h k", k=P), band[:, 0, :],
                                  band[:, 1:2, :].to_broadcast([P, 4, P]), start=True, stop=False)
                        mm = pe.matmul(SC[0][:, b, :], q_s[64 * b:64 * b + 64, :], k_s[64 * b:64 * b + 64, :, :].rearrange("p h k -> p (h k)"),
                                       start=False, stop=True, tile_position=(64 * b, 0))
                    mm.then_inc(S["s_sc"], 1)
                if runs("ffn", i):
                    wait(pe, "ln3_x", n_f)
                    read(("s_done", b_s, 1), ("x_done", b_xo, 1), ("f_logit", b_f, 1))
                    pe.transpose(M0[:, 0:P], xn["ln3"][:], ident[:]).then_inc(S["f_xT_ps"], 1)
                if runs("cross", i):
                    wait(pe, "x_q", n_x)
                    wait(pe, "x_k", n_x)
                    read(("s_k", n_s, 1))
                    read(("s_v", n_s, 1), ("f_base", b_f, 1), ("x_v", b_x, 1), ("x_z", b_x, 2))
                    cross_scores(0)
                if runs("ffn", i):
                    wait(pe, "f_xT", n_f)
                    pe.matmul(M0[:, 0:E], xT_f[:], w_router[:], start=True, stop=True).then_inc(S["f_lg_ps"], 1)
                    read(("f_done", b_f, 1))
                    pe.matmul(M1[:, :], xT_f[:], w_shared[:], start=True, stop=True).then_inc(S["f_gu_ps"], 1)
                if runs("xout", i):
                    wait(pe, "x_e", n_xo, 4)
                    wait(pe, "x_v", n_xo)
                    read(("f_logit", n_f, 1), ("s_done", b_s, 1), ("x_done", b_xo, 1))
                    for part, of in ((0, lambda g, hl: v_x[0:SK, g, hl, :]), (1, lambda g, hl: ones_x[0:SK, hl, :])):
                        for hl in range(4):
                            for g in range(4):
                                mm = pe.matmul(M0[32 * g:32 * g + 32, part * P:(part + 1) * P], of(g, hl), e_x[0:SK, 4 * g + hl, :],
                                               start=(hl == 0), stop=(hl == 3), tile_position=(0, 32 * g))
                    mm.then_inc(S["x_pv"], 1)
                if runs("cross", i):
                    read(("s_z", n_s, 1), ("x_z", b_x, 2))
                    cross_scores(1)
                if runs("self", i):
                    wait(pe, "s_z", n_s)
                    read(("x_e", b_x, 4), ("s_e", b_s, 2))
                    for c in range(2):
                        for j in range(4):
                            mm = pe.transpose(TR[c][:, j * P:(j + 1) * P], z_s[:, 4 * c + j, :], ident[:])
                        mm.then_inc(S["s_tr"], 1)
                if runs("cross", i):
                    wait_part(pe, "x_z", n_x, 2, 0)
                    pe.matmul(M3[0:SK, 0:P], xcT[:, P:P + SK], w_xv[:], start=True, stop=True).then_inc(S["x_v_ps"], 1)
                if runs("xproj", i):
                    wait(pe, "ln2_x", n_xp)
                    wait(pe, "ctx_in", n_xp, 16)
                    if runs("cross", i):
                        wait_part(pe, "x_z", n_x, 2, 0)
                    read(("s_k", n_s, 1), ("x_k", b_xp, 1))
                    pe.transpose(M2[:, 0:P], xn["ln2"][:], ident[:])
                    pe.transpose(M2[:, P:P + SK], ctx_now[:], ident[0:SK, 0:SK]).then_inc(S["x_T_ps"], 1)
                if runs("sproj", i):
                    wait(pe, "ln1_x", n_sp)
                    if isinstance(i, int):
                        wait(pe, "x_k", b_xp)
                        wait(pe, "s_k", b_sp)
                    pe.transpose(M2[:, 256:256 + P], xn["ln1"][:], ident[:]).then_inc(S["s_xT_ps"], 1)
                if runs("xout", i):
                    wait(pe, "x_oT", n_xo)
                    pe.matmul(M0[:, 0:D], oT_x[:], w_xo[:], start=True, stop=True).then_inc(S["x_out_ps"], 1)
                if runs("ffn", i):
                    wait(pe, "f_h", n_f)
                    for c in range(2):
                        mm = pe.transpose(M1[:, c * P:(c + 1) * P], h_f[:, c * P:(c + 1) * P], ident[:])
                    mm.then_inc(S["f_hT_ps"], 1)
                if runs("cross", i):
                    cross_transposes(0)
                    cross_transposes(1)
                if runs("xproj", i):
                    wait(pe, "x_T", n_xp)
                    wait(pe, "s_xT", n_sp)
                    pe.matmul(M2[:, 0:P], w_xq[:], xcT[:, 0:P], start=True, stop=True)
                    pe.matmul(M2[:, P:P + SK], w_xk[:], xcT[:, P:P + SK], start=True, stop=True).then_inc(S["x_qk_ps"], 1)
                if runs("sproj", i):
                    wait(pe, "s_xT", n_sp)
                    wait(pe, "x_T", n_xp)
                    pe.matmul(M2[:, 248:376], w_sq[:], xT_s[:], start=True, stop=True)
                    pe.matmul(M2[:, 376:504], w_sk[:], xT_s[:], start=True, stop=True).then_inc(S["s_qk_ps"], 1)
                if runs("ffn", i):
                    wait(pe, "f_hots", n_f)
                    read(("x_v", n_x, 1), ("s_v", n_s, 1), ("f_base", b_f, 1))
                    pe.matmul(M3[:, 0:E], tri[:, 0, :], hots[:], start=True, stop=True)
                    pe.matmul(M3[:, E:2 * E], tri[:, 1, :], hots[:], start=True, stop=True).then_inc(S["f_rank_ps"], 1)
                if runs("self", i):
                    wait(pe, "s_e", n_s, 2)
                    wait(pe, "s_esink", n_s)
                    wait(pe, "s_v", n_s)
                    read(("x_done", n_xo, 1), ("s_done", b_s, 1), ("f_logit", n_f, 1))
                    for hl in range(2):
                        for g in range(4):
                            pe.matmul(M0[32 * g:32 * g + 32, 0:P], v_s[:, g // 2, hl, :], e_s[:, 2 * g + hl, :],
                                      start=(hl == 0), stop=(hl == 1), tile_position=(0, 32 * g))
                    pe.matmul(M0[:, P:2 * P], esink[:].rearrange("p h d -> p (h d)"), ident[:],
                              start=True, stop=False)
                    for hl in range(2):
                        for g in range(4):
                            mm = pe.matmul(M0[32 * g:32 * g + 32, P:2 * P], ones_s[:, hl, :], e_s[:, 2 * g + hl, :],
                                           start=False, stop=(hl == 1), tile_position=(0, 32 * g))
                    mm.then_inc(S["s_pv"], 1)
                if runs("ffn", i):
                    wait(pe, "f_hT", n_f)
                    pe.matmul(M1[:, 0:D], hT_f[:, 0, :], w_sdown[:, 0, :], start=True, stop=False)
                    pe.matmul(M1[:, 0:D], hT_f[:, 1, :], w_sdown[:, 1, :], start=False, stop=True).then_inc(S["f_dn_ps"], 1)
                if runs("cross", i):
                    cross_transposes(2)
                    cross_transposes(3)
                if runs("sproj", i):
                    read(("f_base", n_f, 1), ("x_v", n_x, 1), ("s_v", b_sp, 1))
                    pe.matmul(M3[:, 0:KV * HD], xT_s[:], w_sv[:], start=True, stop=True).then_inc(S["s_v_ps"], 1)
                if runs("self", i):
                    wait(pe, "s_oT", n_s)
                    pe.matmul(M0[:, 0:D], oT_s[:], w_so[:], start=True, stop=True).then_inc(S["s_out_ps"], 1)

            steps_of(pe, step)

            XT, GU, HT, Y = (PS[:, b, :] for b in range(4))
            pe.wait_ge(S["x_done"], TILES)
            pe.wait_ge(S["f_done"], TILES)
            pe.wait_ge(S["f_base"], TILES)
            pe.wait_ge(S["w_late"], 16 * 3)
            pe.wait_ge(S["w_half"], 2)
            pe.wait_ge(S["t_table"], 1)

            def pair(j, u):
                static = isinstance(j, int)
                down_at, up_at = [], []
                for a in range(2):
                    if not static or 0 <= j - 3 < PAIRS:
                        down_at.append(pe.value_load(at_block(2, j - 3, a), min_val=0, max_val=(E - 1) * D))
                    if not static or 0 <= j - 1 < PAIRS:
                        up_at.append(pe.value_load(at_block(1, j - 1, a), min_val=0, max_val=(E - 1) * 2 * EH))
                if not static or 0 <= j - 3 < PAIRS:
                    pe.wait_ge(S["e_hT"], j - 2)
                    if not static or j - 3 > 0:
                        pe.wait_ge(S["e_y"], j - 3)
                    for a in range(2):
                        mm = pe.matmul(Y[:, a * D:(a + 1) * D], hT_e[:, a, :], w_down[:].rearrange("p e n -> p (e n)")[:, bass.ds(down_at[a], D)],
                                       start=True, stop=True)
                    mm.then_inc(S["e_y_ps"], 1)
                if not static or 0 <= j - 2 < PAIRS:
                    pe.wait_ge(S["e_h"], j - 1)
                    if not static or j - 2 > 0:
                        pe.wait_ge(S["e_hT"], j - 2)
                    for a in range(2):
                        mm = pe.transpose(HT[:, a * P:(a + 1) * P], h_e[:, a, :], ident[:])
                    mm.then_inc(S["e_hT_ps"], 1)
                if not static or 0 <= j - 1 < PAIRS:
                    pe.wait_ge(S["e_xT"], j)
                    if not static or j - 1 > 0:
                        pe.wait_ge(S["e_h"], j - 1)
                    for a in range(2):
                        mm = pe.matmul(GU[:, a * 2 * EH:(a + 1) * 2 * EH], xT_e[:, a, :],
                                       w_up[:].rearrange("p e n -> p (e n)")[:, bass.ds(up_at[a], 2 * EH)], start=True, stop=True)
                    mm.then_inc(S["e_gu_ps"], 1)
                if not static or 0 <= j < PAIRS:
                    if static:
                        pe.wait_ge(S[f"e_in{u}"], 32 * (j // RING + 1))
                        if j > 0:
                            pe.wait_ge(S["e_xT"], j)
                    else:
                        pe.wait_ge(S[f"e_in{u}"], (j - u) * (32 // RING) + 32)
                        pe.wait_ge(S["e_xT"], j)
                    for a in range(2):
                        mm = pe.transpose(XT[:, a * P:(a + 1) * P], rows_in[:, u, a, 0:D], ident[:])
                    mm.then_inc(S["e_xT_ps"], 1)

            pairs_of(pe, pair)

        @block.scalar
        def _(act):
            act.wait_ge(S["w_early"], 16 * (EARLY + 3))
            nc.scalar.mul(b_q4, b_q, 1.0 / HD ** 0.5).then_inc(S["b_ready"], 1)
            nc.scalar.mul(bk_half[:], half_s, b_k).then_inc(S["b_ready"], 1)
            nc.scalar.mul(bxk_half[:], half_x, bx_k).then_inc(S["b_ready"], 1)
            act.wait_ge(S["b_ready"], 3)

            def step(i):
                n_sp, n_s, n_xp, n_x, n_f = (done(s, i) for s in ("sproj", "self", "xproj", "cross", "ffn"))
                b_f = before("ffn", i)

                def normed(ln, ago, *waits):
                    wait(act, ln + "_shift", done(ln, i - ago))
                    for name, n, per in waits:
                        wait(act, name, n, per)
                    nc.scalar.activation(xn[ln][:, 0:D], tile(X, ln, i - ago), ACT.Identity, bias=shift[ln][:], scale=rstd[ln][:]).then_inc(S[ln + "_x"], 1)

                def cross_exp(c):
                    wait_part(act, "x_tr", n_x, 4, c)
                    nc.scalar.activation(e_x[0:SK, 4 * c:4 * c + 4, :], TR[c % 2][0:SK, :].rearrange("p (h q) -> p h q", q=P),
                                         ACT.Exp, scale=1.0 / XD ** 0.5).then_inc(S["x_e"], 1)

                if runs("ffn", i):
                    wait(act, "f_xT_ps", n_f)
                    wait(act, "f_gu_ps", b_f)
                    nc.scalar.copy(xT_f[:], M0[:, 0:P]).then_inc(S["f_xT"], 1)
                if runs("self", i):
                    wait(act, "s_max", n_s)
                    wait(act, "s_tr", before("self", i), 2)
                    for h in range(H):
                        z = nc.scalar.activation(z_s[:, h, :], SC[0][:, h // 4, (h % 4) * P:(h % 4 + 1) * P], ACT.Identity, bias=nmax_s[:, h:h + 1])
                    z.then_inc(S["s_z"], 1)
                if runs("ffn", i):
                    wait(act, "f_gu_ps", n_f)
                    wait(act, "f_g", b_f)
                    nc.scalar.activation(th_f[:], M1[:, 0:SH], ACT.Tanh, scale=0.5).then_inc(S["f_th"], 1)
                if runs("xproj", i):
                    normed("ln2", 1, ("x_T_ps", before("xproj", i), 1))
                if runs("self", i):
                    wait(act, "s_pv", before("self", i))
                    nc.scalar.activation(esink[:], nmax_s[:].rearrange("p (h a) -> p h a", a=1).to_broadcast([P, H, HD]), ACT.Exp, bias=sink).then_inc(S["s_esink"], 1)
                if runs("ffn", i):
                    wait(act, "f_top", n_f)
                    nc.scalar.activation(tile(GATE, "ffn", i), top[:, 0:2], ACT.Tanh, scale=0.5).then_inc(S["f_gate"], 1)
                if runs("self", i):
                    for c in range(2):
                        wait_part(act, "s_tr", n_s, 2, c)
                        nc.scalar.activation(e_s[:, 4 * c:4 * c + 4, :], TR[c].rearrange("p (h q) -> p h q", q=P), ACT.Exp).then_inc(S["s_e"], 1)
                if runs("xproj", i):
                    wait(act, "x_T_ps", n_xp)
                    wait(act, "s_xT_ps", n_sp)
                    wait(act, "x_v_ps", n_x)
                    nc.scalar.copy(xcT[:], M2[:, 0:P + SK]).then_inc(S["x_T"], 1)
                if runs("sproj", i):
                    wait(act, "s_xT_ps", n_sp)
                    wait(act, "x_T_ps", n_xp)
                    wait(act, "s_v_ps", before("sproj", i))
                    nc.scalar.copy(xT_s[:], M2[:, 256:256 + P]).then_inc(S["s_xT"], 1)
                if runs("ffn", i):
                    wait(act, "f_hT_ps", n_f)
                    wait(act, "f_dn_ps", b_f)
                    nc.scalar.copy(hT_f[:].rearrange("p c q -> p (c q)"), M1[:, 0:2 * P]).then_inc(S["f_hT"], 1)
                if runs("cross", i):
                    wait(act, "x_pv", before("cross", i))
                    cross_exp(0)
                    cross_exp(1)
                if runs("xproj", i):
                    wait(act, "x_qk_ps", n_xp)
                    wait(act, "s_qk_ps", n_sp)
                    wait(act, "x_sc", n_x, 2)
                    nc.scalar.activation(q_x[:], M2[:, 0:P], ACT.Identity, bias=bx_q).then_inc(S["x_q"], 1)
                    for h in range(4):
                        k = nc.scalar.activation(k_x[:, h, :], M2[:, P:P + SK], ACT.Identity, bias=bxk_half[:, h:h + 1], scale=half_x[:, h:h + 1])
                    k.then_inc(S["x_k"], 1)
                if runs("sproj", i):
                    wait(act, "s_qk_ps", n_sp)
                    wait(act, "s_sc", n_s)
                    nc.scalar.activation(q_s[:], M2[:, 248:376], ACT.Identity, bias=b_q4, scale=1.0 / HD ** 0.5).then_inc(S["s_q"], 1)
                    for h in range(4):
                        k = nc.scalar.activation(k_s[:, h, :], M2[:, 376:504], ACT.Identity, bias=bk_half[:, h:h + 1], scale=half_s[:, h:h + 1])
                    k.then_inc(S["s_k"], 1)
                if runs("cross", i):
                    cross_exp(2)
                    cross_exp(3)
                if runs("ln1", i):
                    normed("ln1", 0, ("s_xT_ps", before("ln1", i), 1))
                if runs("ln3", i):
                    normed("ln3", 0, ("f_xT_ps", before("ln3", i), 1), ("ln3_sent", before("ln3", i), 1))

            steps_of(act, step)

            XT, GU, HT, Y = (PS[:, b, :] for b in range(4))

            def pair(j, u):
                static = isinstance(j, int)
                if not static or 0 <= j - 2 < PAIRS:
                    pe_n = j - 1
                    act.wait_ge(S["e_hT_ps"], pe_n)
                    if not static or j - 2 > 0:
                        act.wait_ge(S["e_y_ps"], j - 2)
                    nc.scalar.copy(hT_e[:].rearrange("p a q -> p (a q)"), HT[:, 0:2 * P]).then_inc(S["e_hT"], 1)
                if not static or 0 <= j - 1 < PAIRS:
                    act.wait_ge(S["e_gu_ps"], j)
                    if not static or j - 1 > 0:
                        act.wait_ge(S["e_g"], j - 1)
                    nc.scalar.activation(th_e[:], GU.rearrange("p (a n) -> p a n", a=2)[:, :, 0:EH], ACT.Tanh, scale=0.5).then_inc(S["e_th"], 1)
                if not static or 0 <= j < PAIRS:
                    act.wait_ge(S["e_xT_ps"], j + 1)
                    if not static or j > 0:
                        act.wait_ge(S["e_gu_ps"], j)
                    nc.scalar.copy(xT_e[:].rearrange("p a q -> p (a q)"), XT[:, 0:2 * P]).then_inc(S["e_xT"], 1)

            pairs_of(act, pair)

            with act.Fori(0, TILES) as t:
                act.wait_ge(S["g_done"], t + 1)
                act.dma_start(out[bass.ds(t, 1), :, :].rearrange("a p d -> p a d"), X[:, bass.ds(t, 1), :]).then_inc(S["g_out"], 16)
            act.wait_ge(S["g_out"], 16 * TILES)

        @block.vector
        def _(dve):
            nc.vector.memset(minus_half[:], -0.5).then_inc(S["s_const"], 1)
            nc.vector.memset(v_s[:], 0.0).then_inc(S["s_const"], 1)
            nc.vector.memset(v_x[:], 0.0).then_inc(S["s_const"], 1)
            nc.vector.memset(ones_s[:], 0.0).then_inc(S["s_const"], 1)
            nc.vector.memset(ones_x[:], 0.0).then_inc(S["s_const"], 1)
            dve.wait_ge(S["s_const"], 5)
            for hl in range(2):
                nc.vector.memset(ones_s[:, hl, hl * HD:(hl + 1) * HD], 1.0).then_inc(S["s_const"], 1)
            for hl in range(4):
                nc.vector.memset(ones_x[:, hl, hl * XD:(hl + 1) * XD], 1.0).then_inc(S["s_const"], 1)
            dve.wait_ge(S["w_early"], 16 * (EARLY + 3))
            nc.vector.tensor_copy(base[:], base0).then_inc(S["s_const"], 1)
            nc.vector.tensor_scalar(minus_sink[:], sink, -1.0, None, ALU.mult).then_inc(S["s_const"], 1)
            dve.wait_ge(S["s_const"], CONSTANTS)

            def statistics(ln, i, *waits):
                met(dve)
                for name, n, per in waits:
                    wait(dve, name, n, per)
                wait(dve, ln + "_mv", before(ln, i))
                nc.vector.bn_stats(stats[ln][:], tile(X, ln, i)).then_inc(S[ln + "_stats"], 1)

            def aggregate(ln, i):
                met(dve)
                wait(dve, ln + "_stats", done(ln, i))
                wait(dve, ln + "_x", before(ln, i))
                nc.vector.bn_aggr(mv[ln][:], stats[ln][:]).then_inc(S[ln + "_mv"], 1)

            def step(i):
                n_s, n_x, n_xo, n_f = (done(s, i) for s in ("self", "cross", "xout", "ffn"))
                b_f = before("ffn", i)

                def cross_max(half):
                    wait_part(dve, "x_sc", n_x, 2, half)
                    nc.vector.tensor_reduce(max_x[:, 8 * half:8 * half + 8], SC[1 - half][:, :, 0:4 * SK].rearrange("p b (h k) -> p b h k", k=SK),
                                            AX.X, ALU.max).then_inc(S["x_max"], 1)

                def cross_less(half):
                    part = slice(8 * half, 8 * half + 8)
                    wait_part(dve, "x_max", n_x, 2, half)
                    wait(dve, "x_tr", before("cross", i), 4)
                    nc.vector.tensor_tensor(z_x[:, part, :].rearrange("p (b h) k -> p b h k", b=2),
                                            SC[1 - half][:, :, 0:4 * SK].rearrange("p b (h k) -> p b h k", k=SK),
                                            max_x[:, part].rearrange("p (b h a) -> p b h a", b=2, a=1).to_broadcast([P, 2, 4, SK]),
                                            ALU.subtract).then_inc(S["x_z"], 1)

                if runs("self", i):
                    wait(dve, "s_sc", n_s)
                    wait(dve, "s_max", before("self", i))
                    nc.vector.tensor_reduce(rowmax[:], SC[0].rearrange("p b (h k) -> p (b h) k", k=P), AX.X, ALU.max, negate=True).then_inc(S["s_rowmax"], 1)
                    wait(dve, "s_rowmax", n_s)
                    wait(dve, "s_z", before("self", i))
                    wait(dve, "s_esink", before("self", i))
                    nc.vector.tensor_scalar(nmax_s[:], rowmax[:], minus_sink[:], None, ALU.min).then_inc(S["s_max"], 1)
                if runs("cross", i):
                    cross_max(0)
                if runs("ffn", i):
                    wait(dve, "f_lg_ps", n_f)
                    wait(dve, "f_topi", b_f)
                    nc.vector.tensor_copy(logit[:], M0[:, 0:E]).then_inc(S["f_logit"], 1)
                if runs("cross", i):
                    cross_less(0)
                if runs("ffn", i):
                    met(dve)
                    wait(dve, "f_logit", n_f)
                    wait(dve, "f_gate", b_f)
                    nc.vector.max(top[:], logit[:]).then_inc(S["f_top"], 1)
                    wait(dve, "f_th", n_f)
                    nc.vector.scalar_tensor_tensor(out=g_f[:], in0=th_f[:], scalar=1.0, in1=M1[:, 0:SH], op0=ALU.add, op1=ALU.mult).then_inc(S["f_g"], 1)
                    met(dve)
                    wait(dve, "f_top", n_f)
                    nc.vector.max_index(top_i[:], top[:], logit[:]).then_inc(S["f_topi"], 1)
                    wait(dve, "f_g", n_f)
                    wait(dve, "f_hT_ps", b_f)
                    nc.vector.tensor_tensor(h_f[:], M1[:, SH:2 * SH], g_f[:], ALU.mult).then_inc(S["f_h"], 1)
                    wait(dve, "f_topi", n_f)
                    nc.vector.tensor_copy(top_f[:], top_i[:, 0:2]).then_inc(S["f_topf"], 1)
                if runs("xout", i):
                    wait(dve, "x_pv", n_xo)
                    wait(dve, "x_oT", before("xout", i))
                    nc.vector.reciprocal(rden_x[:], M0[:, P:2 * P]).then_inc(S["x_rden"], 1)
                if runs("ffn", i):
                    wait(dve, "f_topf", n_f)
                    nc.vector.tensor_tensor(hot[:], iota_e.rearrange("p (a e) -> p a e", a=1).to_broadcast([P, 2, E]),
                                            top_f[:].rearrange("p (s a) -> p s a", a=1).to_broadcast([P, 2, E]), ALU.is_equal).then_inc(S["f_hot"], 1)
                if runs("xout", i):
                    wait(dve, "x_rden", n_xo)
                    wait(dve, "x_out_ps", before("xout", i))
                    nc.vector.tensor_tensor(oT_x[:], M0[:, 0:P], rden_x[:], ALU.mult).then_inc(S["x_oT"], 1)
                if runs("ffn", i):
                    wait(dve, "f_hot", n_f)
                    wait(dve, "f_rank_ps", b_f)
                    nc.vector.tensor_tensor(hots[:], hot[:, 0, :], hot[:, 1, :], ALU.add).then_inc(S["f_hots"], 1)
                if runs("ln1", i):
                    statistics("ln1", i, ("x_in", done("ln1", i), 16))
                if runs("cross", i):
                    cross_max(1)
                if runs("ln1", i):
                    aggregate("ln1", i)
                if runs("cross", i):
                    cross_less(1)
                    wait(dve, "x_v_ps", n_x)
                    wait(dve, "x_pv", n_xo)
                    nc.vector.tensor_tensor(own_block(v_x), M3[0:SK, 0:P].rearrange("p (g h d) -> p g h d", g=4, h=4),
                                            bx_v[0:SK, :].rearrange("p (g h d) -> p g h d", g=4, h=4), ALU.add).then_inc(S["x_v"], 1)
                if runs("xout", i):
                    wait(dve, "x_out_ps", n_xo)
                    wait(dve, "x_xb", n_xo)
                    nc.vector.tensor_tensor(tile(X, "xout", i), M0[:, 0:D], xb_x[:], ALU.add).then_inc(S["x_done"], 1)
                if runs("ffn", i):
                    wait(dve, "f_rank_ps", n_f)
                    wait(dve, "f_pick", b_f)
                    nc.vector.tensor_tensor(place[:], M3[:, 0:E], base[:], ALU.add).then_inc(S["f_place"], 1)
                if runs("ln3", i):
                    statistics("ln3", i, ("x_done", done("ln3", i), 1))
                if runs("ffn", i):
                    wait(dve, "f_place", n_f)
                    nc.vector.tensor_tensor(base[:], M3[:, E:2 * E], base[:], ALU.add).then_inc(S["f_base"], 1)
                if runs("ln3", i):
                    aggregate("ln3", i)
                if runs("ffn", i):
                    nc.vector.tensor_tensor(picked[:], hot[:], place[:].rearrange("p (a e) -> p a e", a=1).to_broadcast([P, 2, E]),
                                            ALU.mult).then_inc(S["f_pick"], 1)
                    wait(dve, "f_pick", n_f)
                    nc.vector.tensor_reduce(row_f[:], picked[:], AX.X, ALU.add).then_inc(S["f_rowf"], 1)
                    wait(dve, "f_rowf", n_f)
                    wait(dve, "f_sent", b_f, 32)
                    nc.vector.tensor_copy(row_i[:], row_f[:]).then_inc(S["f_row"], 1)
                if runs("self", i):
                    wait(dve, "s_pv", n_s)
                    wait(dve, "s_oT", before("self", i))
                    nc.vector.reciprocal(rden_s[:], M0[:, P:2 * P]).then_inc(S["s_rden"], 1)
                    wait(dve, "s_rden", n_s)
                    wait(dve, "s_out_ps", before("self", i))
                    nc.vector.tensor_tensor(oT_s[:], M0[:, 0:P], rden_s[:], ALU.mult).then_inc(S["s_oT"], 1)
                if runs("ffn", i):
                    wait(dve, "f_dn_ps", n_f)
                    nc.vector.tensor_tensor(tile(X, "ffn", i), M1[:, 0:D], tile(X, "ffn", i), ALU.add).then_inc(S["f_done"], 1)
                if runs("sproj", i):
                    wait(dve, "s_v_ps", done("sproj", i))
                    wait(dve, "s_pv", n_s)
                    for hl in range(2):
                        v = nc.vector.tensor_tensor(v_s[:, :, hl, hl * HD:(hl + 1) * HD], M3[:, 0:KV * HD].rearrange("p (h d) -> p h d", h=KV),
                                                    b_v[:].rearrange("p (h d) -> p h d", h=KV), ALU.add)
                    v.then_inc(S["s_v"], 1)
                if runs("self", i):
                    wait(dve, "s_out_ps", n_s)
                    wait(dve, "s_xb", n_s)
                    nc.vector.tensor_tensor(tile(X, "self", i), M0[:, 0:D], xb_s[:], ALU.add).then_inc(S["s_done"], 1)
                if runs("ln2", i):
                    statistics("ln2", i, ("s_done", n_s, 1))
                    aggregate("ln2", i)

            steps_of(dve, step)

            chain = [0]

            def link(ins):
                chain[0] += 1
                ins.then_inc(S["t_step"], 1)
                dve.wait_ge(S["t_step"], chain[0])

            dve.wait_ge(S["w_late"], 16 * 3)
            dve.wait_ge(S["f_base"], TILES)
            nc.vector.tensor_copy(tail[:], base[0:1, :]).then_inc(S["t_tail"], 1)
            link(nc.vector.tensor_tensor(count[:], base[:], base0, ALU.subtract))
            link(nc.vector.tensor_tensor(full[:], count[:].rearrange("p (e a) -> p e a", a=1).to_broadcast([P, E, TILES]),
                                         steps.rearrange("p (a n) -> p a n", a=1).to_broadcast([P, E, TILES]), ALU.is_gt))
            link(nc.vector.tensor_reduce(n_blk[:], full[:], AX.X, ALU.add))
            link(nc.vector.tensor_copy(ends[:, 0:1], n_blk[:, 0:1]))
            for e in range(1, E):
                link(nc.vector.tensor_tensor(ends[:, e:e + 1], ends[:, e - 1:e], n_blk[:, e:e + 1], ALU.add))
            blk = blocks[:].rearrange("p (t a) -> p t a", a=1).to_broadcast([1, BLOCKS, E])
            link(nc.vector.tensor_tensor(past[:], blk, ends[0:1, :].rearrange("p (a e) -> p a e", a=1).to_broadcast([1, BLOCKS, E]), ALU.is_ge))
            link(nc.vector.tensor_reduce(of[:], past[:], AX.X, ALU.add))
            link(nc.vector.tensor_tensor(past[:], past[:], n_blk[0:1, :].rearrange("p (a e) -> p a e", a=1).to_broadcast([1, BLOCKS, E]), ALU.mult))
            link(nc.vector.tensor_reduce(at[:], past[:], AX.X, ALU.add))
            link(nc.vector.tensor_tensor(at[:], blocks[:], at[:], ALU.subtract))
            link(nc.vector.tensor_scalar(at[:], at[:], float(P), None, ALU.mult))
            link(nc.vector.tensor_scalar(off_f[:, 0, :], of[:], float(REGION), None, ALU.mult))
            link(nc.vector.tensor_tensor(off_f[:, 0, :], off_f[:, 0, :], at[:], ALU.add))
            link(nc.vector.tensor_scalar(of[:], of[:], float(E - 1), None, ALU.min))
            link(nc.vector.tensor_scalar(off_f[:, 1, :], of[:], float(2 * EH), None, ALU.mult))
            link(nc.vector.tensor_scalar(off_f[:, 2, :], of[:], float(D), None, ALU.mult))
            nc.vector.tensor_copy(table[:], off_f[:]).then_inc(S["t_table"], 1)
            XT, GU, HT, Y = (PS[:, b, :] for b in range(4))
            gu = GU.rearrange("p (a n) -> p a n", a=2)

            def pair(j, u):
                static = isinstance(j, int)
                if not static or 0 <= j - 3 < PAIRS:
                    dve.wait_ge(S["e_y_ps"], j - 2)
                    w = (u - 3) % RING
                    if not static:
                        dve.wait_ge(S[f"e_out{w}"], (j - u) * (32 // RING) - (32 if u < 3 else 0))
                    elif j - 3 >= RING:
                        dve.wait_ge(S[f"e_out{w}"], (j - 3) // RING * 32)
                    nc.vector.tensor_copy(rows_out[:, w, :, :].rearrange("p a d -> p (a d)"), Y[:, 0:2 * D]).then_inc(S["e_y"], 1)
                if not static or 0 <= j - 1 < PAIRS:
                    dve.wait_ge(S["e_th"], j)
                    nc.vector.scalar_tensor_tensor(out=g_e[:], in0=th_e[:], scalar=1.0, in1=gu[:, :, 0:EH], op0=ALU.add, op1=ALU.mult).then_inc(S["e_g"], 1)
                    dve.wait_ge(S["e_g"], j)
                    if not static or j - 1 > 0:
                        dve.wait_ge(S["e_hT_ps"], j - 1)
                    nc.vector.tensor_tensor(h_e[:], gu[:, :, EH:2 * EH], g_e[:], ALU.mult).then_inc(S["e_h"], 1)

            pairs_of(dve, pair)

            dve.wait_ge(S["f_gate"], TILES)
            nc.vector.tensor_scalar(GATE[:], GATE[:], 0.5, 0.5, ALU.mult, ALU.add).then_inc(S["g_gate"], 1)
            dve.wait_ge(S["g_gate"], 1)
            with dve.Fori(0, TILES // GRING) as r:
                for u in range(GRING):
                    t = r * GRING
                    x_t = X[:, bass.ds(t + u, 1), :].rearrange("p a d -> p (a d)")
                    gate = GATE[:, bass.ds(t + u, 1), :].rearrange("p a s -> p (a s)")
                    dve.wait_ge(S[f"g_back{u}"], r * 16 + 16)
                    nc.vector.scalar_tensor_tensor(out=summed[:, u, :], in0=back[:, u, 0, :], scalar=gate[:, 0:1], in1=x_t,
                                                   op0=ALU.mult, op1=ALU.add).then_inc(S["g_sum"], 1)
                    dve.wait_ge(S["g_sum"], t + (u + 1))
                    nc.vector.scalar_tensor_tensor(out=x_t, in0=back[:, u, 1, :], scalar=gate[:, 1:2], in1=summed[:, u, :],
                                                   op0=ALU.mult, op1=ALU.add).then_inc(S["g_done"], 1)

        @block.gpsimd
        def _(pool):
            pool.wait_ge(S["s_const"], CONSTANTS)
            pool.wait_ge(S["w_early"], 16 * (EARLY + 3))
            nc.gpsimd.tensor_scalar(w_sdown[:], w_sdown[:], 0.5, 1.0, ALU.mult, ALU.mult).then_inc(S["w_half"], 1)

            def root(ln, i):
                n, last = done(ln, i), before(ln, i)
                wait(pool, ln + "_mv", n)
                wait(pool, ln + "_rstd", last)
                passed(pool)
                nc.gpsimd.tensor_scalar(var[ln][:], mv[ln][:, 1:2], EPS, 1.0, ALU.add, ALU.mult).then_inc(S[ln + "_var"], 1)
                wait(pool, ln + "_x", last)
                wait(pool, ln + "_var", n)
                nc.gpsimd.tensor_tensor(rstd[ln][:], var[ln][:], minus_half[:], ALU.pow).then_inc(S[ln + "_rstd"], 1)
                wait(pool, ln + "_rstd", n)
                passed(pool)
                nc.gpsimd.tensor_scalar(shift[ln][:], mv[ln][:, 0:1], -1.0, rstd[ln][:], ALU.mult, ALU.mult).then_inc(S[ln + "_shift"], 1)

            def step(i):
                if runs("ffn", i):
                    wait(pool, "ln3_x", done("ffn", i))
                    wait(pool, "f_sent", before("ffn", i), 32)
                    passed(pool)
                    nc.gpsimd.tensor_copy(rows_sent[:, :, 0:D], xn["ln3"][:].rearrange("p (a d) -> p a d", a=1).to_broadcast([P, 2, D])).then_inc(S["ln3_sent"], 1)
                    nc.gpsimd.tensor_copy(rows_sent[:, :, D:W].bitcast(U32), tile(dest, "ffn", i).rearrange("p (s a) -> p s a", a=1)).then_inc(S["ln3_dest"], 1)
                if runs("xout", i):
                    wait(pool, "x_done", before("xout", i))
                    nc.gpsimd.tensor_tensor(xb_x[:], tile(X, "xout", i), bx_o[:], ALU.add).then_inc(S["x_xb"], 1)
                if runs("self", i):
                    wait(pool, "x_in", done("self", i), 16)
                    wait(pool, "s_done", before("self", i))
                    nc.gpsimd.tensor_tensor(xb_s[:], tile(X, "self", i), b_o[:], ALU.add).then_inc(S["s_xb"], 1)
                if runs("ln1", i):
                    root("ln1", i)
                if runs("ln3", i):
                    root("ln3", i)
                if runs("ffn", i):
                    wait(pool, "f_row", done("ffn", i))
                    wait(pool, "ln3_sent", done("ffn", i))
                    wait(pool, "ln3_dest", done("ffn", i))
                    passed(pool)
                    for s in range(2):
                        nc.gpsimd.indirect_dma_start(sent[:, :], bass.IndirectOffsetOnAxis(row_i[:, s:s + 1], 0), rows_sent[:, s, :], None).then_inc(S["f_sent"], 16)
                if runs("ln2", i):
                    root("ln2", i)

            steps_of(pool, step)
            pool.wait_ge(S["w_late"], 16 * 3)
            nc.gpsimd.tensor_scalar(w_down[:], w_down[:], 0.5, 1.0, ALU.mult, ALU.mult).then_inc(S["w_half"], 1)
            with pool.Fori(0, PAIRS // RING) as r:
                for u in range(RING):
                    pool.wait_ge(S["e_y"], r * RING + (u + 1))
                    passed(pool)
                    for a in range(2):
                        nc.gpsimd.indirect_dma_start(made[:, :], bass.IndirectOffsetOnAxis(rows_in[:, u, a, D:W].bitcast(U32), 0),
                                                     rows_out[:, u, a, :], None).then_inc(S[f"e_out{u}"], 16)


def kernel(**inputs):
    import concourse.bacc as bacc
    from concourse.bass_utils import run_bass_kernel_spmd

    a = {n: np.asarray(v) for n, v in inputs.items()}
    arrays = {
        "x": a["x"], "ctx": a["ctx_1024"], "sink": a["L0_attn_sink_bias"].reshape(1),
        "wq": a["L0_attn_Wq"].T, "wk": a["L0_attn_Wk"].T, "wv": a["L0_attn_Wv"].T, "wo": a["L0_attn_Wo"].T,
        "bq": a["L0_attn_bq"], "bk": a["L0_attn_bk"], "bv": a["L0_attn_bv"], "bo": a["L0_attn_bo"],
        "xwq": a["L0_xattn_wq"].T, "xwk": a["L0_xattn_wk"].T, "xwv": a["L0_xattn_wv"].T, "xwo": a["L0_xattn_wo"].T,
        "xbq": a["L0_xattn_bq"], "xbk": a["L0_xattn_bk"], "xbv": a["L0_xattn_bv"], "xbo": a["L0_xattn_bo"],
        "router": a["L0_ffn_router_w"].T, "gate_up": a["L0_ffn_gate_up_w"], "down": a["L0_ffn_down_w"],
        "shared_gate": a["L0_ffn_shared_gate_w"].T, "shared_up": a["L0_ffn_shared_up_w"].T, "shared_down": a["L0_ffn_shared_down_w"].T,
    }
    arrays.update(constants())
    arrays = {n: np.ascontiguousarray(v) for n, v in arrays.items()}
    nc = bacc.Bacc("TRN2", target_bir_lowering=False, num_devices=1)
    aps = {n: nc.dram_tensor(n, v.shape, mybir.dt.from_np(v.dtype), kind="ExternalInput").ap() for n, v in arrays.items()}
    out = nc.dram_tensor("out", [TILES, P, D], F32, kind="ExternalOutput").ap()
    decoder_program(nc, aps, out)
    r = run_bass_kernel_spmd(nc, [arrays], core_ids=[0])
    return r.results[0]["out"]
```

```python
from contextlib import ExitStack

import numpy as np

import concourse.bass as bass
from concourse import mybir

F32 = mybir.dt.float32
F16 = mybir.dt.float16
U32 = mybir.dt.uint32
I32 = mybir.dt.int32
ALU = mybir.AluOpType
ACT = mybir.ActivationFunctionType
AX = mybir.AxisListType

TILES, P, D = 64, 128, 128
SK = 120
H, KV, HD = 8, 2, 16
WIN = 32
XH, XD = 16, 8
E, EH = 16, 128
SH = 256
EPS = 1e-5
FP16_MIN = -65504.0
REGION = TILES * P + P
DUMMY = E * REGION
BLOCKS = (2 * TILES * P + E * (P - 1)) // P + 1
PAIRS = BLOCKS // 2
SPARE = BLOCKS - 2 * TILES
ROWS = DUMMY + SPARE * P
W = D + 1
TOKENS = TILES * P
PLACES = ROWS // P
assert ROWS % P == 0 and PLACES * PLACES <= 1 << 24
RING = 8
GRING = 8

SKEW = {"ln1": -2, "sproj": -1, "self": 0, "ln2": 0, "xproj": 1, "cross": 2, "xout": 3, "ln3": 3, "ffn": 4}
FIRST_STEP, LAST_STEP = -2, TILES + 3
AHEAD = 4
CONSTANTS = 16
EARLY = 6
LOOP_FROM, LOOP_TO = 5, TILES - 2


PACKS = {
    "first": (("ident", P), ("small", 64), ("bq", 1), ("bk", 1), ("xbq", 1), ("xbk", 1), ("sink", 1), ("bv", KV * HD), ("bo", D), ("wq", P), ("wk", P), ("wv", KV * HD)),
    "second": (("wo", D), ("xbv", D), ("xbo", D), ("xwq", D), ("xwk", D), ("xwv", D), ("xwo", D), ("router", E)),
    "third": (("shared", 2 * SH), ("shared_down", 2 * D)),
}


def constants():
    p = np.arange(P)
    r = np.arange(2 * WIN)
    band = (r[None, :] <= p[:, None] % WIN + WIN) & (r[None, :] > p[:, None] % WIN) & (r[None, :] + (p[:, None] // WIN - 1) * WIN >= 0)
    small = np.zeros((P, 64), np.float32)
    small[:, 0:2] = 2 * p[:, None] + np.arange(2)
    small[:, 42] = np.where(p < TILES, p * P, 2 * TOKENS)
    small[:, 38:42] = (p[:, None] % 64 // HD) == np.arange(4)
    small[:, 2:6] = (p[:, None] % 32 // XD) == np.arange(4)
    small[:, 6:22] = np.arange(E)
    small[:, 22:38] = np.arange(E) * REGION
    return {
        "c_band": np.concatenate([np.eye(P), np.where(band, 0.0, FP16_MIN)], 1).astype(np.float16),
        "c_tri": np.concatenate([p[:, None] < p[None, :], np.ones((P, P))], 1).astype(np.float16),
        "small": small, "ident": np.eye(P, dtype=np.float32),
        "c_dest": (2 * (np.arange(TILES)[None, :, None] * P + p[:, None, None]) + np.arange(2)).astype(np.uint32),
        "c_fill": np.concatenate([np.zeros(((E + SPARE) * P, D)), 2 * TOKENS + np.arange((E + SPARE) * P)[:, None]], 1).astype(np.uint32),
    }


def decoder_program(nc, A, out):
    sent = nc.dram_tensor("sent_rows", [ROWS, W], F32, kind="Internal").ap()
    made = nc.dram_tensor("made_rows", [2 * TOKENS + (E + SPARE) * P, D], F32, kind="Internal").ap()

    with ExitStack() as ctx:
        def sb(name, shape, dt=F32):
            return ctx.enter_context(nc.sbuf_tensor(name, shape, dt))

        def sem(name):
            return ctx.enter_context(nc.semaphore(name))

        X = sb("X", [P, TILES, D])
        ctx_now = sb("ctx_now", [SK, D])
        packs_sb = {name: sb("pack_" + name, [P, sum(n for _, n in parts)]) for name, parts in PACKS.items()}
        part = {}
        for name, parts in PACKS.items():
            at_col = 0
            for member, n in parts:
                part[member] = packs_sb[name][:, at_col:at_col + n]
                at_col += n
        w_sq, w_sk, w_sv, w_so, w_xq, w_xk, w_xv, w_xo = (part[n] for n in "wq wk wv wo xwq xwk xwv xwo".split())
        w_router, w_shared, ident, small = part["router"], part["shared"], part["ident"], part["small"]
        w_sdown = part["shared_down"].rearrange("p (c d) -> p c d", c=2)
        b_q, b_k, bx_q, bx_k, sink, b_v, b_o, bx_v, bx_o = (part[n] for n in "bq bk xbq xbk sink bv bo xbv xbo".split())
        b_q4 = sb("b_q4", [P, 1])
        w_up = sb("w_up", [P, E, 2 * EH])
        w_down = sb("w_down", [P, E, D])
        band = sb("band", [P, P + 2 * WIN], F16); tri = sb("tri", [P, 2, P], F16)
        half_s, half_x, iota_e, base0 = small[:, 38:42], small[:, 2:6], small[:, 6:22], small[:, 22:38]
        block_no, step_no = small[:, 0:2], small[:, 42:43]
        minus_half = sb("minus_half", [P, 1])
        dest = sb("dest", [P, TILES, 2], U32)
        bk_half = sb("bk_half", [P, 4]); bxk_half = sb("bxk_half", [P, 4]); minus_sink = sb("minus_sink", [P, 1])
        ones_s = sb("ones_s", [P, 32]); ones_x = sb("ones_x", [P, 4, 32])
        stats = {n: sb(f"stats_{n}", [P, 6]) for n in ("ln1", "ln2", "ln3")}
        mv = {n: sb(f"mv_{n}", [P, 2]) for n in ("ln1", "ln2", "ln3")}
        var = {n: sb(f"var_{n}", [P, 1]) for n in ("ln1", "ln2", "ln3")}
        rstd = {n: sb(f"rstd_{n}", [P, 1]) for n in ("ln1", "ln2", "ln3")}
        xn = {n: sb(f"xn_{n}", [P, D]) for n in ("ln1", "ln2", "ln3")}
        shift = {n: sb(f"shift_{n}", [P, 1]) for n in ("ln1", "ln2", "ln3")}
        rows_sent = sb("rows_sent", [P, 2, W])
        xT_s = sb("xT_s", [P, WIN + P]); q_s = sb("q_s", [P, P]); k_s = sb("k_s", [P, 4, WIN + P])
        v_s = sb("v_s", [P, P // WIN, KV, 32])
        rowmax = sb("rowmax", [P, H]); nmax_s = sb("nmax_s", [P, H]); esink = sb("esink", [P, H, HD]); z_s = sb("z_s", [P, H, 2 * WIN]); e_s = sb("e_s", [P, H // 2, P])
        rden_s = sb("rden_s", [P, P]); oT_s = sb("oT_s", [P, P]); xb_s = sb("xb_s", [P, D])
        xcT = sb("xcT", [P, P + SK]); q_x = sb("q_x", [P, P]); k_x = sb("k_x", [P, 4, SK])
        v_x = sb("v_x", [P, 4, 4, 32])
        max_x = sb("max_x", [P, XH]); z_x = sb("z_x", [P, XH, SK]); e_x = sb("e_x", [P, XH, P])
        rden_x = sb("rden_x", [P, P]); oT_x = sb("oT_x", [P, P]); xb_x = sb("xb_x", [P, D])
        xT_f = sb("xT_f", [P, P]); th_f = sb("th_f", [P, SH]); g_f = sb("g_f", [P, SH]); h_f = sb("h_f", [P, SH]); hT_f = sb("hT_f", [P, 2, P])
        logit = sb("logit", [P, E]); top = sb("top", [P, 8]); top_i = sb("top_i", [P, 8], U32); top_f = sb("top_f", [P, 2])
        hot = sb("hot", [P, 2, E]); hots = sb("hots", [P, E], F16); base = sb("base", [P, E]); place = sb("place", [P, E])
        picked = sb("picked", [P, 2, E]); row_f = sb("row_f", [P, 2]); row_i = sb("row_i", [P, 2], U32)
        GATE = sb("GATE", [P, TILES, 2])
        count = sb("count", [P, E]); full = sb("full", [P, E], F16)
        ends = sb("ends", [P, 2, 2 * E])
        past = sb("past", [P, 2, E]); of = sb("of", [P, 2]); at = sb("at", [P, 2])
        region_at = sb("region_at", [P, 2]); entries = sb("entries", [P, 2]); table = sb("table", [1, 2, PAIRS], I32)
        tail = sb("tail", [1, E], I32)
        rows_in = sb("rows_in", [P, RING, 2, W]); xT_e = sb("xT_e", [P, 2, P]); th_e = sb("th_e", [P, 2, EH])
        g_e = sb("g_e", [P, 2, EH]); h_e = sb("h_e", [P, 2, 2, EH]); hT_e = sb("hT_e", [P, 2, P]); rows_out = sb("rows_out", [P, RING, 2, D])
        back = sb("back", [P, GRING, 2, 2, D]); summed = sb("summed", [P, GRING, 2, D])

        PS = ctx.enter_context(nc.psum_tensor("PS", [P, 8, 512], F32))
        SC = [PS[:, 0:2, :], PS[:, 2:4, :]]
        TR = [PS[:, 4, :], PS[:, 5, :]]
        M0, M1, M2, M3 = (PS[:, b, :] for b in (6, 7, 2, 3))

        names = """w_early w_late s_const b_ready x_in ctx_in zeroed passed
            ln1_stats ln1_mv ln1_var ln1_shift ln1_rstd ln1_x ln2_stats ln2_mv ln2_var ln2_rstd ln2_shift ln2_x
            ln3_stats ln3_mv ln3_var ln3_shift ln3_rstd ln3_x ln3_dest ln3_sent
            s_xT_ps s_xT s_qk_ps s_q s_k s_v_ps s_v s_sc s_rowmax s_max s_z s_esink s_tr s_e s_pv s_rden s_oT s_out_ps s_xb s_done
            x_T_ps x_T x_qk_ps x_q x_k x_v_ps x_v x_sc x_max x_z x_tr x_e x_pv x_rden x_oT x_out_ps x_xb x_done
            f_xT_ps f_xT f_lg_ps f_logit f_top f_topi f_topf f_hot f_hots f_gate f_gu_ps f_th f_g f_h f_rank_ps f_place f_base f_pick f_rowf f_row f_sent
            f_hT_ps f_hT f_dn_ps f_done
            t_step t_full t_blocks t_offsets t_rows t_table t_tail w_half e_xT_ps e_xT e_gu_ps e_th e_g e_h e_hT_ps e_hT e_y_ps e_y
            g_gate g_sum g_done g_out""".split()
        S = {n: sem(n) for n in names}
        for u in range(RING):
            S[f"e_in{u}"] = sem(f"e_in{u}")
            S[f"e_out{u}"] = sem(f"e_out{u}")
        for n in range(E // 2):
            S[f"tail{n}"] = sem(f"tail{n}")
        assert E // 2 <= RING
        for u in range(GRING):
            S[f"g_back{u}"] = sem(f"g_back{u}")

        def entry(row, j):
            return table[0:1, row, j:j + 1] if isinstance(j, int) else table[0:1, row, bass.ds(j, 1)]

        def steps_of(eng, body):
            for i in range(FIRST_STEP, LOOP_FROM):
                body(i)
            with eng.Fori(LOOP_FROM, LOOP_TO) as i:
                body(i)
            for i in range(LOOP_TO, LAST_STEP + 1):
                body(i)

        def runs(stage, i):
            return not isinstance(i, int) or 0 <= i - SKEW[stage] < TILES

        def done(stage, i):
            n = i - SKEW[stage] + 1
            return max(0, min(TILES, n)) if isinstance(i, int) else n

        def before(stage, i):
            return done(stage, i - 1)

        def wait(eng, name, n, per=1):
            if isinstance(n, int) and n <= 0:
                return
            eng.wait_ge(S[name], n * per if per != 1 else n)

        def tile(buf, stage, i):
            t = i - SKEW[stage]
            return buf[:, t, :] if isinstance(t, int) else buf[:, bass.ds(t, 1), :].rearrange("p a d -> p (a d)")

        def passed(eng):
            eng.sem_inc(S["passed"], 1)

        def met(eng):
            eng.wait_ge(S["s_const"], CONSTANTS)

        def wait_part(eng, name, n, parts, c):
            eng.wait_ge(S[name], n * parts - (parts - 1 - c))

        def pairs_of(eng, body):
            for j in range(2 * RING):
                body(j, j % RING)
            with eng.Fori(2, PAIRS // RING) as r:
                for u in range(RING):
                    body(r * RING + u, u)
            for j in range(PAIRS, PAIRS + 3):
                body(j, j % RING)

        def own_block(v):
            a = v[0:SK]
            return bass.AP(tensor=a.tensor, offset=a.offset, ap=[[4 * 4 * 32, SK], [4 * 32, 4], [32 + XD, 4], [1, XD]])

        def fill_tail(eng, e):
            r = eng.value_load(tail[0:1, e:e + 1], min_val=0, max_val=DUMMY - P)
            eng.dma_start(sent[bass.ds(r, P), :], A["c_fill"][e * P:(e + 1) * P, :].bitcast(F32)).then_inc(S[f"tail{e // 2}"], 16)

        block = ctx.enter_context(nc.Block())

        @block.sync
        def _(sp):
            for dst, src in ((packs_sb["first"], A["first"]), (packs_sb["second"], A["second"])):
                sp.dma_start(dst[:], src).then_inc(S["w_early"], 16)
            for t in range(AHEAD):
                sp.dma_start(X[:, t, :], A["x"][t, :, :]).then_inc(S["x_in"], 16)
                sp.wait_ge(S["x_in"], t * 16 + 16)
            for dst, src in ((w_up, A["gate_up"].rearrange("e p n -> p e n")), (w_down, A["down"].rearrange("e p n -> p e n"))):
                sp.dma_start(dst[:], src).then_inc(S["w_late"], 16)
            sp.dma_start(ctx_now[:], A["ctx"][0, :, :]).then_inc(S["ctx_in"], 16)
            with sp.Fori(1, TILES - AHEAD + 1) as t:
                sp.dma_start(X[:, bass.ds(t + (AHEAD - 1), 1), :], A["x"][bass.ds(t + (AHEAD - 1), 1), :, :].rearrange("a p d -> p a d")).then_inc(S["x_in"], 16)
                sp.wait_ge(S["x_T_ps"], t)
                sp.dma_start(ctx_now[:], A["ctx"][bass.ds(t, 1), :, :].rearrange("a p d -> p (a d)")).then_inc(S["ctx_in"], 16)
                sp.wait_ge(S["x_in"], t * 16 + AHEAD * 16)
                passed(sp)
            for t in range(TILES - AHEAD + 1, TILES):
                sp.wait_ge(S["x_T_ps"], t)
                sp.dma_start(ctx_now[:], A["ctx"][t, :, :]).then_inc(S["ctx_in"], 16)
            for b in range(SPARE):
                sp.dma_start(sent[DUMMY + b * P:DUMMY + (b + 1) * P, :], A["c_fill"][(E + b) * P:(E + b + 1) * P, :].bitcast(F32)).then_inc(S["zeroed"], 16)
            sp.wait_ge(S["zeroed"], 16 * SPARE)
            sp.wait_ge(S["t_tail"], 1)
            for e in range(0, E // 2, 2):
                fill_tail(sp, e)
            sp.wait_ge(S["f_sent"], 32 * TILES)
            sp.wait_ge(S["t_table"], 1)

            def load(j, u):
                both = sp.value_load(entry(0, j), min_val=0, max_val=PLACES * PLACES - 1)
                for a, r in enumerate((both % PLACES, both // PLACES)):
                    sp.dma_start(rows_in[:, u, a, :], sent[bass.ds(r * P, P), :]).then_inc(S[f"e_in{u}"], 16)

            for j in range(RING):
                if j < E // 2:
                    sp.wait_ge(S[f"tail{j}"], 32)
                load(j, j)
                if E // 2 + 2 * j < E:
                    fill_tail(sp, E // 2 + 2 * j)
            with sp.Fori(1, PAIRS // RING) as r:
                for u in range(RING):
                    sp.wait_ge(S[f"e_out{u}"], r * 32)
                    load(r * RING + u, u)
            for u in range(RING):
                sp.wait_ge(S[f"e_out{u}"], 32 * (PAIRS // RING))

            def fetch(n, u):
                src = made[n * 4 * P:(n + 1) * 4 * P, :] if isinstance(n, int) else made[bass.ds(n * (4 * P), 4 * P), :]
                sp.dma_start(back[:, u, :, :, :].rearrange("p t s d -> p t (s d)"), src.rearrange("(t p s) d -> p t (s d)", t=2, s=2)).then_inc(S[f"g_back{u}"], 16)

            for n in range(GRING):
                fetch(n, n)
            with sp.Fori(1, TILES // 2 // GRING) as r:
                for u in range(GRING):
                    sp.wait_ge(S["g_done"], r * (2 * GRING) + (2 * u + 2 - 2 * GRING))
                    fetch(r * GRING + u, u)

        @block.tensor
        def _(pe):
            pe.wait_ge(S["w_early"], 16 * EARLY)

            pe.wait_ge(S["w_half"], 1)

            def step(i):
                n_sp, n_s, n_xp, n_x, n_xo, n_f = (done(s, i) for s in ("sproj", "self", "xproj", "cross", "xout", "ffn"))
                b_sp, b_s, b_xp, b_x, b_xo, b_f = (before(s, i) for s in ("sproj", "self", "xproj", "cross", "xout", "ffn"))

                def read(*readers):
                    for name, n, per in readers[:1] if not isinstance(i, int) else readers:
                        wait(pe, name, n, per)

                def cross_scores(half):
                    for b in range(2):
                        g = 2 * half + b
                        mm = pe.matmul(SC[1 - half][:, b, 0:4 * SK], q_x[32 * g:32 * g + 32, :],
                                       k_x[32 * g:32 * g + 32, :, :].rearrange("p h k -> p (h k)"),
                                       start=True, stop=True, tile_position=(32 * g, 0))
                    mm.then_inc(S["x_sc"], 1)

                def cross_transposes(c):
                    wait_part(pe, "x_z", n_x, 2, c // 2)
                    if c < 2:
                        read(*((("s_e", n_s, 1),) if c == 1 else ()), ("x_e", b_x, 4))
                    else:
                        wait_part(pe, "x_e", n_x, 4, c - 2)
                    for j in range(4):
                        mm = pe.transpose(TR[c % 2][0:SK, j * P:(j + 1) * P], z_x[:, 4 * c + j, :], ident[:])
                    mm.then_inc(S["x_tr"], 1)

                if runs("self", i):
                    wait(pe, "s_q", n_s)
                    wait(pe, "s_k", n_s)
                    read(("x_z", b_x, 2), ("s_z", b_s, 1))
                    for kv in range(KV):
                        scores = SC[0][:, kv, 0:4 * 2 * WIN].rearrange("p (h k) -> p h k", k=2 * WIN)
                        pe.matmul(scores, band[:, 0:P], band[:, P:].rearrange("p (a k) -> p a k", a=1).to_broadcast([P, 4, 2 * WIN]), start=True, stop=False)
                        for b in range(0, P, WIN):
                            mm = pe.matmul(scores[b:b + WIN], q_s[64 * kv:64 * kv + 64, b:b + WIN],
                                           k_s[64 * kv:64 * kv + 64, :, b:b + 2 * WIN], start=False, stop=True, tile_position=(64 * kv, b))
                    mm.then_inc(S["s_sc"], 1)
                if runs("cross", i):
                    wait(pe, "x_q", n_x)
                    wait(pe, "x_k", n_x)
                    read(("s_k", n_s, 1))
                    read(("s_v", n_s, 1), ("f_base", b_f, 1), ("x_v", b_x, 1), ("x_z", b_x, 2))
                    cross_scores(0)
                if runs("ffn", i):
                    wait(pe, "ln3_x", n_f)
                    read(("f_done", b_f, 1))
                    pe.transpose(M1[:, 0:P], xn["ln3"][:], ident[:]).then_inc(S["f_xT_ps"], 1)
                if runs("xout", i):
                    wait(pe, "x_e", n_xo, 4)
                    wait(pe, "x_v", n_xo)
                    read(("s_done", b_s, 1), ("x_done", b_xo, 1))
                    for part, of in ((0, lambda g, hl: v_x[0:SK, g, hl, :]), (1, lambda g, hl: ones_x[0:SK, hl, :])):
                        for hl in range(4):
                            for g in range(4):
                                mm = pe.matmul(M0[32 * g:32 * g + 32, part * P:(part + 1) * P], of(g, hl), e_x[0:SK, 4 * g + hl, :],
                                               start=(hl == 0), stop=(hl == 3), tile_position=(0, 32 * g))
                    mm.then_inc(S["x_pv"], 1)
                if runs("ffn", i):
                    wait(pe, "f_xT", n_f)
                    pe.matmul(M1[:, 0:E], xT_f[:], w_router[:], start=True, stop=True).then_inc(S["f_lg_ps"], 1)
                if runs("cross", i):
                    read(("s_z", n_s, 1), ("x_z", b_x, 2))
                    cross_scores(1)
                if runs("ffn", i):
                    wait(pe, "f_logit", n_f)
                    pe.matmul(M1[:, :], xT_f[:], w_shared[:], start=True, stop=True).then_inc(S["f_gu_ps"], 1)
                if runs("self", i):
                    wait(pe, "s_z", n_s)
                    read(("x_e", b_x, 4), ("s_e", b_s, 1))
                    for g in range(H // 2):
                        mm = pe.transpose(TR[1][:, g * P:(g + 1) * P], z_s[:, 2 * g:2 * g + 2, :].rearrange("p h k -> p (h k)"), ident[:])
                    mm.then_inc(S["s_tr"], 1)
                if runs("cross", i):
                    wait_part(pe, "x_z", n_x, 2, 0)
                    pe.matmul(M3[0:SK, 0:P], xcT[:, P:P + SK], w_xv[:], start=True, stop=True).then_inc(S["x_v_ps"], 1)
                if runs("xproj", i):
                    wait(pe, "ln2_x", n_xp)
                    wait(pe, "ctx_in", n_xp, 16)
                    if runs("cross", i):
                        wait_part(pe, "x_z", n_x, 2, 0)
                    read(("s_k", n_s, 1), ("x_k", b_xp, 1))
                    pe.transpose(M2[:, 0:P], xn["ln2"][:], ident[:])
                    pe.transpose(M2[:, P:P + SK], ctx_now[:], ident[0:SK, 0:SK]).then_inc(S["x_T_ps"], 1)
                if runs("sproj", i):
                    wait(pe, "ln1_x", n_sp)
                    if isinstance(i, int):
                        wait(pe, "x_k", b_xp)
                        wait(pe, "s_k", b_sp)
                    pe.transpose(M2[:, 256:256 + P], xn["ln1"][:], ident[:]).then_inc(S["s_xT_ps"], 1)
                if runs("xout", i):
                    wait(pe, "x_oT", n_xo)
                    pe.matmul(M0[:, 0:D], oT_x[:], w_xo[:], start=True, stop=True).then_inc(S["x_out_ps"], 1)
                if runs("cross", i):
                    cross_transposes(0)
                    cross_transposes(1)
                if runs("xproj", i):
                    wait(pe, "x_T", n_xp)
                    wait(pe, "s_xT", n_sp)
                    pe.matmul(M2[:, 0:P], w_xq[:], xcT[:, 0:P], start=True, stop=True)
                    pe.matmul(M2[:, P:P + SK], w_xk[:], xcT[:, P:P + SK], start=True, stop=True).then_inc(S["x_qk_ps"], 1)
                if runs("sproj", i):
                    wait(pe, "s_xT", n_sp)
                    wait(pe, "x_T", n_xp)
                    pe.matmul(M2[:, 248:376], w_sq[:], xT_s[:, WIN:], start=True, stop=True)
                    pe.matmul(M2[:, 376:504], w_sk[:], xT_s[:, WIN:], start=True, stop=True).then_inc(S["s_qk_ps"], 1)
                if runs("ffn", i):
                    wait(pe, "f_hots", n_f)
                    read(("x_v", n_x, 1), ("s_v", n_s, 1), ("f_base", b_f, 1))
                    pe.matmul(M3[:, 0:E], tri[:, 0, :], hots[:], start=True, stop=True)
                    pe.matmul(M3[:, E:2 * E], tri[:, 1, :], hots[:], start=True, stop=True).then_inc(S["f_rank_ps"], 1)
                if runs("self", i):
                    wait(pe, "s_e", n_s)
                    wait(pe, "s_esink", n_s)
                    wait(pe, "s_v", n_s)
                    read(("x_done", n_xo, 1), ("s_done", b_s, 1))
                    for b in range(P // WIN):
                        for g in range(4):
                            pe.matmul(M0[32 * g:32 * g + 32, b * WIN:(b + 1) * WIN], v_s[:, b, g // 2, :], e_s[:, g, b * WIN:(b + 1) * WIN],
                                      start=True, stop=True, tile_position=(0, 32 * g))
                    pe.matmul(M0[:, P:2 * P], esink[:].rearrange("p h d -> p (h d)"), ident[:],
                              start=True, stop=False)
                    for g in range(4):
                        mm = pe.matmul(M0[32 * g:32 * g + 32, P:2 * P], ones_s[:], e_s[:, g, :],
                                       start=False, stop=True, tile_position=(0, 32 * g))
                    mm.then_inc(S["s_pv"], 1)
                if runs("ffn", i):
                    wait(pe, "f_h", n_f)
                    for c in range(2):
                        mm = pe.transpose(M1[:, c * P:(c + 1) * P], h_f[:, c * P:(c + 1) * P], ident[:])
                    mm.then_inc(S["f_hT_ps"], 1)
                if runs("cross", i):
                    cross_transposes(2)
                if runs("sproj", i):
                    read(("f_base", n_f, 1), ("x_v", n_x, 1), ("s_v", b_sp, 1))
                    for b in range(P // WIN):
                        for hl in range(2):
                            mm = pe.matmul(M3[64 * hl:64 * hl + 64, b * KV * HD:(b + 1) * KV * HD], xT_s[:, b * WIN:(b + 2) * WIN], w_sv[:],
                                           start=True, stop=True, tile_position=(0, 64 * hl))
                    mm.then_inc(S["s_v_ps"], 1)
                if runs("ffn", i):
                    wait(pe, "f_hT", n_f)
                    pe.matmul(M1[:, 0:D], hT_f[:, 0, :], w_sdown[:, 0, :], start=True, stop=False)
                    pe.matmul(M1[:, 0:D], hT_f[:, 1, :], w_sdown[:, 1, :], start=False, stop=True).then_inc(S["f_dn_ps"], 1)
                if runs("self", i):
                    wait(pe, "s_oT", n_s)
                    pe.matmul(M0[:, 0:D], oT_s[:], w_so[:], start=True, stop=True).then_inc(S["s_out_ps"], 1)
                if runs("cross", i):
                    cross_transposes(3)

            steps_of(pe, step)

            pe.wait_ge(S["t_full"], 1)
            pe.matmul(M3[:, 0:E], tri[:, 1, :], full[:], start=True, stop=True).then_inc(S["t_blocks"], 1)
            pe.wait_ge(S["t_offsets"], 1)
            for r in range(2):
                mm = pe.transpose(M2[0:1, r * PAIRS:(r + 1) * PAIRS], entries[0:PAIRS, r:r + 1], ident[0:PAIRS, 0:PAIRS])
            mm.then_inc(S["t_rows"], 1)

            XT, HT = PS[:, 0, :], PS[:, 1, :]
            Y = [PS[:, 4, :], PS[:, 7, :]]
            GU = [PS[:, 5, :], PS[:, 6, :]]
            pe.wait_ge(S["x_done"], TILES)
            pe.wait_ge(S["f_done"], TILES)
            pe.wait_ge(S["f_base"], TILES)
            pe.wait_ge(S["w_late"], 16 * 2)
            pe.wait_ge(S["w_half"], 2)
            pe.wait_ge(S["t_table"], 1)

            expert_at = {}

            def look_up(j, u, ago):
                if isinstance(j, int) and not 0 <= j + ago < PAIRS:
                    return
                if u + ago not in expert_at:
                    both = pe.value_load(entry(1, j + ago), min_val=0, max_val=E * E - 1)
                    expert_at[u + ago] = [both % E, both // E]

            def pair(j, u):
                static = isinstance(j, int)
                if static or u == 0:
                    expert_at.clear()
                look_up(j, u, -1)
                if not static or 0 <= j - 1 < PAIRS:
                    pe.wait_ge(S["e_xT"], j)
                    if not static or j - 1 > 1:
                        pe.wait_ge(S["e_h"], j - 2)
                    for a in range(2):
                        mm = pe.matmul(GU[(u - 1) % 2][:, a * 2 * EH:(a + 1) * 2 * EH], xT_e[:, a, :],
                                       w_up[:].rearrange("p e n -> p (e n)")[:, bass.ds(expert_at[u - 1][a] * (2 * EH), 2 * EH)], start=True, stop=True)
                    mm.then_inc(S["e_gu_ps"], 1)
                look_up(j, u, -3)
                if not static and u + 1 < RING:
                    look_up(j, u, 0)
                if not static or 0 <= j < PAIRS:
                    if static:
                        pe.wait_ge(S[f"e_in{u}"], 32 * (j // RING + 1))
                        if j > 0:
                            pe.wait_ge(S["e_xT"], j)
                    else:
                        pe.wait_ge(S[f"e_in{u}"], (j - u) * (32 // RING) + 32)
                        pe.wait_ge(S["e_xT"], j)
                    for a in range(2):
                        mm = pe.transpose(XT[:, a * P:(a + 1) * P], rows_in[:, u, a, 0:D], ident[:])
                    mm.then_inc(S["e_xT_ps"], 1)
                if not static or 0 <= j - 3 < PAIRS:
                    pe.wait_ge(S["e_hT"], j - 2)
                    if not static or j - 4 > 0:
                        pe.wait_ge(S["e_y"], j - 4)
                    for a in range(2):
                        mm = pe.matmul(Y[(u - 3) % 2][:, a * D:(a + 1) * D], hT_e[:, a, :], w_down[:].rearrange("p e n -> p (e n)")[:, bass.ds(expert_at[u - 3][a] * D, D)],
                                       start=True, stop=True)
                    mm.then_inc(S["e_y_ps"], 1)
                if not static or 0 <= j - 2 < PAIRS:
                    pe.wait_ge(S["e_h"], j - 1)
                    if not static or j - 2 > 0:
                        pe.wait_ge(S["e_hT"], j - 2)
                    for a in range(2):
                        mm = pe.transpose(HT[:, a * P:(a + 1) * P], h_e[:, (u - 2) % 2, a, :], ident[:])
                    mm.then_inc(S["e_hT_ps"], 1)

            pairs_of(pe, pair)

        @block.scalar
        def _(act):
            for dst, src in ((band, A["c_band"]), (packs_sb["third"], A["third"]),
                             (tri, A["c_tri"].rearrange("p (a b) -> p a b", a=2)), (dest, A["c_dest"])):
                act.dma_start(dst[:], src).then_inc(S["w_early"], 16)
            act.wait_ge(S["w_early"], 16 * EARLY)
            nc.scalar.mul(b_q4[:], b_q, 1.0 / HD ** 0.5).then_inc(S["b_ready"], 1)
            nc.scalar.mul(bk_half[:], half_s, b_k).then_inc(S["b_ready"], 1)
            nc.scalar.mul(bxk_half[:], half_x, bx_k).then_inc(S["b_ready"], 1)
            act.wait_ge(S["b_ready"], 3)

            def step(i):
                n_sp, n_s, n_xp, n_x, n_f = (done(s, i) for s in ("sproj", "self", "xproj", "cross", "ffn"))
                b_f = before("ffn", i)

                def normed(ln, ago, *waits):
                    wait(act, ln + "_shift", done(ln, i - ago))
                    for name, n, per in waits:
                        wait(act, name, n, per)
                    nc.scalar.activation(xn[ln][:, 0:D], tile(X, ln, i - ago), ACT.Identity, bias=shift[ln][:], scale=rstd[ln][:]).then_inc(S[ln + "_x"], 1)

                def cross_exp(c):
                    wait_part(act, "x_tr", n_x, 4, c)
                    nc.scalar.activation(e_x[0:SK, 4 * c:4 * c + 4, :], TR[c % 2][0:SK, :].rearrange("p (h q) -> p h q", q=P),
                                         ACT.Exp, scale=1.0 / XD ** 0.5).then_inc(S["x_e"], 1)

                if runs("ffn", i):
                    wait(act, "f_xT_ps", n_f)
                    wait(act, "f_gu_ps", b_f)
                    nc.scalar.copy(xT_f[:], M1[:, 0:P]).then_inc(S["f_xT"], 1)
                if runs("self", i):
                    wait(act, "s_max", n_s)
                    wait(act, "s_tr", before("self", i))
                    for h in range(H):
                        z = nc.scalar.activation(z_s[:, h, :], SC[0][:, h // 4, (h % 4) * 2 * WIN:(h % 4 + 1) * 2 * WIN], ACT.Identity, bias=nmax_s[:, h:h + 1])
                    z.then_inc(S["s_z"], 1)
                if runs("xproj", i):
                    normed("ln2", 1, ("x_T_ps", before("xproj", i), 1))
                if runs("self", i):
                    wait(act, "s_max", n_s)
                    wait(act, "s_pv", before("self", i))
                    nc.scalar.activation(esink[:], nmax_s[:].rearrange("p (h a) -> p h a", a=1).to_broadcast([P, H, HD]), ACT.Exp, bias=sink).then_inc(S["s_esink"], 1)
                if runs("ffn", i):
                    wait(act, "f_top", n_f)
                    nc.scalar.activation(tile(GATE, "ffn", i), top[:, 0:2], ACT.Tanh, scale=0.5).then_inc(S["f_gate"], 1)
                if runs("ffn", i):
                    wait(act, "f_gu_ps", n_f)
                    wait(act, "f_g", b_f)
                    nc.scalar.activation(th_f[:], M1[:, 0:SH], ACT.Tanh, scale=0.5).then_inc(S["f_th"], 1)
                if runs("self", i):
                    wait(act, "s_tr", n_s)
                    nc.scalar.activation(e_s[:], TR[1].rearrange("p (g q) -> p g q", q=P), ACT.Exp).then_inc(S["s_e"], 1)
                if runs("xproj", i):
                    wait(act, "x_T_ps", n_xp)
                    wait(act, "s_xT_ps", n_sp)
                    wait(act, "x_v_ps", n_x)
                    nc.scalar.copy(xcT[:], M2[:, 0:P + SK]).then_inc(S["x_T"], 1)
                if runs("sproj", i):
                    wait(act, "s_xT_ps", n_sp)
                    wait(act, "x_T_ps", n_xp)
                    wait(act, "s_v_ps", before("sproj", i))
                    nc.scalar.copy(xT_s[:, WIN:], M2[:, 256:256 + P]).then_inc(S["s_xT"], 1)
                if runs("cross", i):
                    wait(act, "x_pv", before("cross", i))
                    cross_exp(0)
                    cross_exp(1)
                if runs("sproj", i):
                    wait(act, "s_qk_ps", n_sp)
                    wait(act, "x_qk_ps", n_xp)
                    wait(act, "s_sc", n_s)
                    nc.scalar.activation(q_s[:], M2[:, 248:376], ACT.Identity, bias=b_q4[:], scale=1.0 / HD ** 0.5).then_inc(S["s_q"], 1)
                    for h in range(4):
                        k = nc.scalar.activation(k_s[:, h, WIN:], M2[:, 376:504], ACT.Identity, bias=bk_half[:, h:h + 1], scale=half_s[:, h:h + 1])
                    k.then_inc(S["s_k"], 1)
                if runs("ffn", i):
                    wait(act, "f_hT_ps", n_f)
                    wait(act, "f_dn_ps", b_f)
                    nc.scalar.copy(hT_f[:].rearrange("p c q -> p (c q)"), M1[:, 0:2 * P]).then_inc(S["f_hT"], 1)
                if runs("xproj", i):
                    wait(act, "x_qk_ps", n_xp)
                    wait(act, "s_qk_ps", n_sp)
                    wait(act, "x_sc", n_x, 2)
                    nc.scalar.activation(q_x[:], M2[:, 0:P], ACT.Identity, bias=bx_q).then_inc(S["x_q"], 1)
                    for h in range(4):
                        k = nc.scalar.activation(k_x[:, h, :], M2[:, P:P + SK], ACT.Identity, bias=bxk_half[:, h:h + 1], scale=half_x[:, h:h + 1])
                    k.then_inc(S["x_k"], 1)
                if runs("cross", i):
                    cross_exp(2)
                    cross_exp(3)
                if runs("ln1", i):
                    normed("ln1", 0, ("s_xT_ps", before("ln1", i), 1))
                if runs("ln3", i):
                    normed("ln3", 0, ("f_xT_ps", before("ln3", i), 1), ("ln3_sent", before("ln3", i), 1))

            steps_of(act, step)

            XT, HT = PS[:, 0, :], PS[:, 1, :]
            GU = [PS[:, 5, :], PS[:, 6, :]]
            act.wait_ge(S["t_tail"], 1)
            for e in range(1, E, 2):
                fill_tail(act, e)

            def pair(j, u):
                static = isinstance(j, int)
                if not static or 0 <= j - 1 < PAIRS:
                    act.wait_ge(S["e_gu_ps"], j)
                    if not static or j - 1 > 0:
                        act.wait_ge(S["e_g"], j - 1)
                    nc.scalar.activation(th_e[:], GU[(u - 1) % 2].rearrange("p (a n) -> p a n", a=2)[:, :, 0:EH], ACT.Tanh, scale=0.5).then_inc(S["e_th"], 1)
                if not static or 0 <= j < PAIRS:
                    act.wait_ge(S["e_xT_ps"], j + 1)
                    if not static or j > 0:
                        act.wait_ge(S["e_gu_ps"], j)
                    nc.scalar.copy(xT_e[:].rearrange("p a q -> p (a q)"), XT[:, 0:2 * P]).then_inc(S["e_xT"], 1)
                if not static or 0 <= j - 2 < PAIRS:
                    act.wait_ge(S["e_hT_ps"], j - 1)
                    if not static or j - 2 > 0:
                        act.wait_ge(S["e_y_ps"], j - 2)
                    nc.scalar.copy(hT_e[:].rearrange("p a q -> p (a q)"), HT[:, 0:2 * P]).then_inc(S["e_hT"], 1)

            pairs_of(act, pair)

            with act.Fori(0, TILES // 2) as n:
                act.wait_ge(S["g_done"], n * 2 + 2)
                act.dma_start(out[bass.ds(n * 2, 2), :, :].rearrange("a p d -> p a d"), X[:, bass.ds(n * 2, 2), :]).then_inc(S["g_out"], 16)
            act.wait_ge(S["g_out"], 16 * (TILES // 2))

        @block.vector
        def _(dve):
            nc.vector.memset(minus_half[:], -0.5).then_inc(S["s_const"], 1)
            nc.vector.memset(v_s[:], 0.0).then_inc(S["s_const"], 1)
            nc.vector.memset(v_x[:], 0.0).then_inc(S["s_const"], 1)
            nc.vector.memset(ones_s[:], 0.0).then_inc(S["s_const"], 1)
            nc.vector.memset(ones_x[:], 0.0).then_inc(S["s_const"], 1)
            nc.vector.memset(ends[:], 0.0).then_inc(S["s_const"], 1)
            nc.vector.memset(k_s[:], 0.0).then_inc(S["s_const"], 1)
            nc.vector.memset(xT_s[:], 0.0).then_inc(S["s_const"], 1)
            dve.wait_ge(S["s_const"], 8)
            for hl in range(2):
                nc.vector.memset(ones_s[64 * hl:64 * hl + 64, hl * HD:(hl + 1) * HD], 1.0).then_inc(S["s_const"], 1)
            for hl in range(4):
                nc.vector.memset(ones_x[:, hl, hl * XD:(hl + 1) * XD], 1.0).then_inc(S["s_const"], 1)
            dve.wait_ge(S["w_early"], 16 * EARLY)
            nc.vector.tensor_copy(base[:], base0).then_inc(S["s_const"], 1)
            nc.vector.tensor_scalar(minus_sink[:], sink, -1.0, None, ALU.mult).then_inc(S["s_const"], 1)
            dve.wait_ge(S["s_const"], CONSTANTS)

            def statistics(ln, i, *waits):
                met(dve)
                for name, n, per in waits:
                    wait(dve, name, n, per)
                wait(dve, ln + "_mv", before(ln, i))
                nc.vector.bn_stats(stats[ln][:], tile(X, ln, i)).then_inc(S[ln + "_stats"], 1)

            def aggregate(ln, i):
                met(dve)
                wait(dve, ln + "_stats", done(ln, i))
                wait(dve, ln + "_x", before(ln, i))
                nc.vector.bn_aggr(mv[ln][:], stats[ln][:]).then_inc(S[ln + "_mv"], 1)

            def step(i):
                n_s, n_x, n_xo, n_f = (done(s, i) for s in ("self", "cross", "xout", "ffn"))
                b_f = before("ffn", i)

                def cross_max(half):
                    wait_part(dve, "x_sc", n_x, 2, half)
                    nc.vector.tensor_reduce(max_x[:, 8 * half:8 * half + 8], SC[1 - half][:, :, 0:4 * SK].rearrange("p b (h k) -> p b h k", k=SK),
                                            AX.X, ALU.max).then_inc(S["x_max"], 1)

                def cross_less(half):
                    part = slice(8 * half, 8 * half + 8)
                    wait_part(dve, "x_max", n_x, 2, half)
                    wait(dve, "x_tr", before("cross", i), 4)
                    nc.vector.tensor_tensor(z_x[:, part, :].rearrange("p (b h) k -> p b h k", b=2),
                                            SC[1 - half][:, :, 0:4 * SK].rearrange("p b (h k) -> p b h k", k=SK),
                                            max_x[:, part].rearrange("p (b h a) -> p b h a", b=2, a=1).to_broadcast([P, 2, 4, SK]),
                                            ALU.subtract).then_inc(S["x_z"], 1)

                if runs("self", i):
                    wait(dve, "s_sc", n_s)
                    wait(dve, "s_max", before("self", i))
                    nc.vector.tensor_reduce(rowmax[:], SC[0][:, :, 0:4 * 2 * WIN].rearrange("p b (h k) -> p b h k", k=2 * WIN), AX.X, ALU.max, negate=True).then_inc(S["s_rowmax"], 1)
                    wait(dve, "s_rowmax", n_s)
                    wait(dve, "s_z", before("self", i))
                    wait(dve, "s_esink", before("self", i))
                    nc.vector.tensor_scalar(nmax_s[:], rowmax[:], minus_sink[:], None, ALU.min).then_inc(S["s_max"], 1)
                if runs("cross", i):
                    cross_max(0)
                    cross_less(0)
                if runs("ffn", i):
                    wait(dve, "f_lg_ps", n_f)
                    wait(dve, "f_topi", b_f)
                    nc.vector.tensor_copy(logit[:], M1[:, 0:E]).then_inc(S["f_logit"], 1)
                if runs("xout", i):
                    wait(dve, "x_pv", n_xo)
                    wait(dve, "x_oT", before("xout", i))
                    nc.vector.reciprocal(rden_x[:], M0[:, P:2 * P]).then_inc(S["x_rden"], 1)
                if runs("xout", i):
                    wait(dve, "x_rden", n_xo)
                    wait(dve, "x_out_ps", before("xout", i))
                    nc.vector.tensor_tensor(oT_x[:], M0[:, 0:P], rden_x[:], ALU.mult).then_inc(S["x_oT"], 1)
                if runs("ffn", i):
                    met(dve)
                    wait(dve, "f_logit", n_f)
                    wait(dve, "f_gate", b_f)
                    nc.vector.max(top[:], logit[:]).then_inc(S["f_top"], 1)
                if runs("ln1", i):
                    statistics("ln1", i, ("x_in", done("ln1", i), 16))
                if runs("ffn", i):
                    met(dve)
                    wait(dve, "f_top", n_f)
                    nc.vector.max_index(top_i[:], top[:], logit[:]).then_inc(S["f_topi"], 1)
                if runs("ln1", i):
                    aggregate("ln1", i)
                if runs("ffn", i):
                    wait(dve, "f_topi", n_f)
                    nc.vector.tensor_copy(top_f[:], top_i[:, 0:2]).then_inc(S["f_topf"], 1)
                if runs("ffn", i):
                    wait(dve, "f_topf", n_f)
                    nc.vector.tensor_tensor(hot[:], iota_e.rearrange("p (a e) -> p a e", a=1).to_broadcast([P, 2, E]),
                                            top_f[:].rearrange("p (s a) -> p s a", a=1).to_broadcast([P, 2, E]), ALU.is_equal).then_inc(S["f_hot"], 1)
                if runs("cross", i):
                    cross_max(1)
                if runs("ffn", i):
                    wait(dve, "f_hot", n_f)
                    wait(dve, "f_rank_ps", b_f)
                    nc.vector.tensor_tensor(hots[:], hot[:, 0, :], hot[:, 1, :], ALU.add).then_inc(S["f_hots"], 1)
                if runs("cross", i):
                    wait(dve, "x_v_ps", n_x)
                    wait(dve, "x_pv", n_xo)
                    nc.vector.tensor_tensor(own_block(v_x), M3[0:SK, 0:P].rearrange("p (g h d) -> p g h d", g=4, h=4),
                                            bx_v[0:SK, :].rearrange("p (g h d) -> p g h d", g=4, h=4), ALU.add).then_inc(S["x_v"], 1)
                if runs("cross", i):
                    cross_less(1)
                if runs("xout", i):
                    wait(dve, "x_out_ps", n_xo)
                    wait(dve, "x_xb", n_xo)
                    nc.vector.tensor_tensor(tile(X, "xout", i), M0[:, 0:D], xb_x[:], ALU.add).then_inc(S["x_done"], 1)
                if runs("ffn", i):
                    wait(dve, "f_th", n_f)
                    wait(dve, "f_h", b_f)
                    nc.vector.scalar_tensor_tensor(out=g_f[:], in0=th_f[:], scalar=1.0, in1=M1[:, 0:SH], op0=ALU.add, op1=ALU.mult).then_inc(S["f_g"], 1)
                if runs("ffn", i):
                    wait(dve, "f_g", n_f)
                    wait(dve, "f_hT_ps", b_f)
                    nc.vector.tensor_tensor(h_f[:], M1[:, SH:2 * SH], g_f[:], ALU.mult).then_inc(S["f_h"], 1)
                if runs("ffn", i):
                    wait(dve, "f_rank_ps", n_f)
                    wait(dve, "f_pick", b_f)
                    nc.vector.tensor_tensor(place[:], M3[:, 0:E], base[:], ALU.add).then_inc(S["f_place"], 1)
                if runs("ln3", i):
                    statistics("ln3", i, ("x_done", done("ln3", i), 1))
                if runs("ffn", i):
                    wait(dve, "f_place", n_f)
                    nc.vector.tensor_tensor(base[:], M3[:, E:2 * E], base[:], ALU.add).then_inc(S["f_base"], 1)
                if runs("ln3", i):
                    aggregate("ln3", i)
                if runs("self", i):
                    wait(dve, "s_pv", n_s)
                    wait(dve, "s_oT", before("self", i))
                    nc.vector.reciprocal(rden_s[:], M0[:, P:2 * P]).then_inc(S["s_rden"], 1)
                if runs("ffn", i):
                    nc.vector.tensor_tensor(picked[:], hot[:], place[:].rearrange("p (a e) -> p a e", a=1).to_broadcast([P, 2, E]),
                                            ALU.mult).then_inc(S["f_pick"], 1)
                if runs("self", i):
                    wait(dve, "s_rden", n_s)
                    wait(dve, "s_out_ps", before("self", i))
                    nc.vector.tensor_tensor(oT_s[:], M0[:, 0:P], rden_s[:], ALU.mult).then_inc(S["s_oT"], 1)
                if runs("ffn", i):
                    wait(dve, "f_pick", n_f)
                    nc.vector.tensor_reduce(row_f[:], picked[:], AX.X, ALU.add).then_inc(S["f_rowf"], 1)
                    wait(dve, "f_rowf", n_f)
                    wait(dve, "f_sent", b_f, 32)
                    nc.vector.tensor_copy(row_i[:], row_f[:]).then_inc(S["f_row"], 1)
                if runs("ffn", i):
                    wait(dve, "f_dn_ps", n_f)
                    nc.vector.tensor_tensor(tile(X, "ffn", i), M1[:, 0:D], tile(X, "ffn", i), ALU.add).then_inc(S["f_done"], 1)
                if runs("sproj", i):
                    wait(dve, "s_v_ps", done("sproj", i))
                    wait(dve, "s_pv", n_s)
                    for hl in range(2):
                        rows = slice(64 * hl, 64 * hl + 64)
                        v = nc.vector.tensor_tensor(v_s[rows, :, :, hl * HD:(hl + 1) * HD], M3[rows, 0:P].rearrange("p (b h d) -> p b h d", h=KV, d=HD),
                                                    b_v[rows, :].rearrange("p (a h d) -> p a h d", a=1, h=KV).to_broadcast([64, P // WIN, KV, HD]), ALU.add)
                    v.then_inc(S["s_v"], 1)
                if runs("self", i):
                    wait(dve, "s_out_ps", n_s)
                    wait(dve, "s_xb", n_s)
                    nc.vector.tensor_tensor(tile(X, "self", i), M0[:, 0:D], xb_s[:], ALU.add).then_inc(S["s_done"], 1)
                if runs("ln2", i):
                    statistics("ln2", i, ("s_done", n_s, 1))
                    aggregate("ln2", i)

            steps_of(dve, step)

            chain = [0]

            def link(ins):
                chain[0] += 1
                ins.then_inc(S["t_step"], 1)
                dve.wait_ge(S["t_step"], chain[0])

            dve.wait_ge(S["w_late"], 16 * 2)
            dve.wait_ge(S["f_base"], TILES)
            nc.vector.tensor_copy(tail[:], base[0:1, :]).then_inc(S["t_tail"], 1)
            link(nc.vector.tensor_tensor(count[:], base[:], base0, ALU.subtract))
            nc.vector.tensor_scalar(full[:], count[:], step_no, None, ALU.is_gt).then_inc(S["t_full"], 1)
            dve.wait_ge(S["t_blocks"], 1)
            link(nc.vector.tensor_copy(ends[:, 0, E:], M3[:, 0:E]))
            back_by, cur = 1, 0
            while back_by < E:
                link(nc.vector.tensor_tensor(ends[:, 1 - cur, E:], ends[:, cur, E:], ends[:, cur, E - back_by:2 * E - back_by], ALU.add))
                back_by, cur = 2 * back_by, 1 - cur
            assert cur == 0
            last = ends[:, 0:1, E:].to_broadcast([P, 2, E])
            link(nc.vector.tensor_tensor(past[:], block_no.rearrange("p (t a) -> p t a", a=1).to_broadcast([P, 2, E]), last, ALU.is_ge))
            link(nc.vector.tensor_reduce(of[:], past[:], AX.X, ALU.add))
            link(nc.vector.tensor_tensor(past[:], past[:], last, ALU.mult))
            link(nc.vector.tensor_reduce(at[:], past[:], AX.X, ALU.max))
            link(nc.vector.tensor_tensor(at[:], block_no, at[:], ALU.subtract))
            link(nc.vector.tensor_scalar(region_at[:], of[:], float(REGION // P), None, ALU.mult))
            link(nc.vector.tensor_tensor(at[:], region_at[:], at[:], ALU.add))
            link(nc.vector.scalar_tensor_tensor(out=entries[:, 0:1], in0=at[:, 1:2], scalar=float(PLACES), in1=at[:, 0:1], op0=ALU.mult, op1=ALU.add))
            link(nc.vector.tensor_scalar(of[:], of[:], float(E - 1), None, ALU.min))
            nc.vector.scalar_tensor_tensor(out=entries[:, 1:2], in0=of[:, 1:2], scalar=float(E), in1=of[:, 0:1], op0=ALU.mult, op1=ALU.add).then_inc(S["t_offsets"], 1)
            dve.wait_ge(S["t_rows"], 1)
            nc.vector.tensor_copy(table[:], M2[0:1, 0:2 * PAIRS].rearrange("p (r j) -> p r j", j=PAIRS)).then_inc(S["t_table"], 1)
            Y = [PS[:, 4, :], PS[:, 7, :]]
            GU = [PS[:, 5, :], PS[:, 6, :]]

            def pair(j, u):
                static = isinstance(j, int)
                if not static or 0 <= j - 1 < PAIRS:
                    gu = GU[(u - 1) % 2].rearrange("p (a n) -> p a n", a=2)
                    dve.wait_ge(S["e_th"], j)
                    if not static or j - 1 > 0:
                        dve.wait_ge(S["e_h"], j - 1)
                    nc.vector.scalar_tensor_tensor(out=g_e[:], in0=th_e[:], scalar=1.0, in1=gu[:, :, 0:EH], op0=ALU.add, op1=ALU.mult).then_inc(S["e_g"], 1)
                    dve.wait_ge(S["e_g"], j)
                    if not static or j - 2 > 0:
                        dve.wait_ge(S["e_hT_ps"], j - 2)
                    nc.vector.tensor_tensor(h_e[:, (u - 1) % 2, :, :], gu[:, :, EH:2 * EH], g_e[:], ALU.mult).then_inc(S["e_h"], 1)
                if not static or 0 <= j - 3 < PAIRS:
                    dve.wait_ge(S["e_y_ps"], j - 2)
                    w = (u - 3) % RING
                    if not static:
                        dve.wait_ge(S[f"e_out{w}"], (j - u) * (32 // RING) - (32 if u < 3 else 0))
                    elif j - 3 >= RING:
                        dve.wait_ge(S[f"e_out{w}"], (j - 3) // RING * 32)
                    nc.vector.tensor_copy(rows_out[:, w, :, :].rearrange("p a d -> p (a d)"), Y[(u - 3) % 2][:, 0:2 * D]).then_inc(S["e_y"], 1)

            pairs_of(dve, pair)

            dve.wait_ge(S["f_gate"], TILES)
            nc.vector.tensor_scalar(GATE[:], GATE[:], 0.5, 0.5, ALU.mult, ALU.add).then_inc(S["g_gate"], 1)
            dve.wait_ge(S["g_gate"], 1)
            with dve.Fori(0, TILES // 2 // GRING) as r:
                for u in range(GRING):
                    first = r * (2 * GRING)
                    x_of = [X[:, bass.ds(first + (2 * u + t), 1), :].rearrange("p a d -> p (a d)") for t in range(2)]
                    gate_of = [GATE[:, bass.ds(first + (2 * u + t), 1), :].rearrange("p a s -> p (a s)") for t in range(2)]
                    dve.wait_ge(S[f"g_back{u}"], r * 16 + 16)
                    for t in range(2):
                        nc.vector.scalar_tensor_tensor(out=summed[:, u, t, :], in0=back[:, u, t, 0, :], scalar=gate_of[t][:, 0:1], in1=x_of[t],
                                                       op0=ALU.mult, op1=ALU.add).then_inc(S["g_sum"], 1)
                    for t in range(2):
                        dve.wait_ge(S["g_sum"], first + (2 * u + t + 1))
                        nc.vector.scalar_tensor_tensor(out=x_of[t], in0=back[:, u, t, 1, :], scalar=gate_of[t][:, 1:2], in1=summed[:, u, t, :],
                                                       op0=ALU.mult, op1=ALU.add).then_inc(S["g_done"], 1)

        @block.gpsimd
        def _(pool):
            pool.wait_ge(S["s_const"], CONSTANTS)
            pool.wait_ge(S["w_early"], 16 * EARLY)
            nc.gpsimd.tensor_scalar(w_sdown[:], w_sdown[:], 0.5, 1.0, ALU.mult, ALU.mult).then_inc(S["w_half"], 1)

            def root(ln, i):
                n, last = done(ln, i), before(ln, i)
                wait(pool, ln + "_mv", n)
                wait(pool, ln + "_rstd", last)
                passed(pool)
                nc.gpsimd.tensor_scalar(var[ln][:], mv[ln][:, 1:2], EPS, 1.0, ALU.add, ALU.mult).then_inc(S[ln + "_var"], 1)
                wait(pool, ln + "_x", last)
                wait(pool, ln + "_var", n)
                nc.gpsimd.tensor_tensor(rstd[ln][:], var[ln][:], minus_half[:], ALU.pow).then_inc(S[ln + "_rstd"], 1)
                wait(pool, ln + "_rstd", n)
                passed(pool)
                nc.gpsimd.tensor_scalar(shift[ln][:], mv[ln][:, 0:1], -1.0, rstd[ln][:], ALU.mult, ALU.mult).then_inc(S[ln + "_shift"], 1)

            def step(i):
                if runs("ffn", i):
                    wait(pool, "ln3_x", done("ffn", i))
                    wait(pool, "f_sent", before("ffn", i), 32)
                    passed(pool)
                    nc.gpsimd.tensor_copy(rows_sent[:, :, 0:D], xn["ln3"][:].rearrange("p (a d) -> p a d", a=1).to_broadcast([P, 2, D])).then_inc(S["ln3_sent"], 1)
                    nc.gpsimd.tensor_copy(rows_sent[:, :, D:W].bitcast(U32), tile(dest, "ffn", i).rearrange("p (s a) -> p s a", a=1)).then_inc(S["ln3_dest"], 1)
                if runs("xout", i):
                    wait(pool, "x_done", before("xout", i))
                    nc.gpsimd.tensor_tensor(xb_x[:], tile(X, "xout", i), bx_o[:], ALU.add).then_inc(S["x_xb"], 1)
                if runs("self", i):
                    wait(pool, "x_in", done("self", i), 16)
                    wait(pool, "s_done", before("self", i))
                    nc.gpsimd.tensor_tensor(xb_s[:], tile(X, "self", i), b_o[:], ALU.add).then_inc(S["s_xb"], 1)
                if runs("ln1", i):
                    root("ln1", i)
                if runs("ln3", i):
                    root("ln3", i)
                if runs("ffn", i):
                    wait(pool, "f_row", done("ffn", i))
                    wait(pool, "ln3_sent", done("ffn", i))
                    wait(pool, "ln3_dest", done("ffn", i))
                    passed(pool)
                    for s in range(2):
                        nc.gpsimd.indirect_dma_start(sent[:, :], bass.IndirectOffsetOnAxis(row_i[:, s:s + 1], 0), rows_sent[:, s, :], None).then_inc(S["f_sent"], 16)
                if runs("ln2", i):
                    root("ln2", i)
                if isinstance(i, int) and i == LOOP_FROM - 1:
                    pool.wait_ge(S["w_late"], 16 * 2)
                    nc.gpsimd.tensor_scalar(w_down[:], w_down[:], 0.5, 1.0, ALU.mult, ALU.mult).then_inc(S["w_half"], 1)

            steps_of(pool, step)
            with pool.Fori(0, PAIRS // RING) as r:
                for u in range(RING):
                    pool.wait_ge(S["e_y"], r * RING + (u + 1))
                    passed(pool)
                    for a in range(2):
                        nc.gpsimd.indirect_dma_start(made[:, :], bass.IndirectOffsetOnAxis(rows_in[:, u, a, D:W].bitcast(U32), 0),
                                                     rows_out[:, u, a, :], None).then_inc(S[f"e_out{u}"], 16)


def kernel(**inputs):
    import concourse.bacc as bacc
    from concourse.bass_utils import run_bass_kernel_spmd

    a = {n: np.asarray(v) for n, v in inputs.items()}
    rows = lambda b: np.tile(b[None, :], (P, 1))
    arrays = {"x": a["x"], "ctx": a["ctx_1024"], "gate_up": a["L0_ffn_gate_up_w"], "down": a["L0_ffn_down_w"]}
    arrays.update(constants())
    by_query = lambda w: np.repeat(w.reshape(KV, HD, -1), H // KV, 0).reshape(H * HD, -1)
    members = {
        "ident": arrays.pop("ident"), "small": arrays.pop("small"),
        "wq": a["L0_attn_Wq"].T, "wk": by_query(a["L0_attn_Wk"]).T, "wv": a["L0_attn_Wv"].T, "wo": a["L0_attn_Wo"].T,
        "bq": a["L0_attn_bq"][:, None], "bk": by_query(a["L0_attn_bk"]), "bv": rows(a["L0_attn_bv"]), "bo": rows(a["L0_attn_bo"]),
        "sink": rows(a["L0_attn_sink_bias"].reshape(1)),
        "xwq": a["L0_xattn_wq"].T, "xwk": a["L0_xattn_wk"].T, "xwv": a["L0_xattn_wv"].T, "xwo": a["L0_xattn_wo"].T,
        "xbq": a["L0_xattn_bq"][:, None], "xbk": a["L0_xattn_bk"][:, None], "xbv": rows(a["L0_xattn_bv"]), "xbo": rows(a["L0_xattn_bo"]),
        "router": a["L0_ffn_router_w"].T,
        "shared": np.concatenate([a["L0_ffn_shared_gate_w"].T, a["L0_ffn_shared_up_w"].T], 1),
        "shared_down": a["L0_ffn_shared_down_w"].T.reshape(2, P, D).transpose(1, 0, 2).reshape(P, 2 * D),
    }
    for name, parts in PACKS.items():
        assert all(members[m].shape == (P, n) for m, n in parts)
        arrays[name] = np.concatenate([members[m] for m, _ in parts], 1)
    arrays = {n: np.ascontiguousarray(v) for n, v in arrays.items()}
    nc = bacc.Bacc("TRN2", target_bir_lowering=False, num_devices=1)
    aps = {n: nc.dram_tensor(n, v.shape, mybir.dt.from_np(v.dtype), kind="ExternalInput").ap() for n, v in arrays.items()}
    out = nc.dram_tensor("out", [TILES, P, D], F32, kind="ExternalOutput").ap()
    decoder_program(nc, aps, out)
    r = run_bass_kernel_spmd(nc, [arrays], core_ids=[0])
    return r.results[0]["out"]
```
